# Optimizing a Trainium2 kernel written in Bass

```python
import numpy as np
import jax
import jax.numpy as jnp

def _softmax(x, axis=-1):
    return jax.nn.softmax(x, axis=axis)

def _gelu(x):
    return jax.nn.gelu(x, approximate=True)

def _silu(x):
    return jax.nn.silu(x)

def _sigmoid(x):
    return jax.nn.sigmoid(x)

def _layernorm(x, axis=-1, eps=1e-05):
    m = jnp.mean(x, axis=axis, keepdims=True)
    v = jnp.var(x, axis=axis, keepdims=True)
    return (x - m) / jnp.sqrt(v + eps)

def _scatter_add(tgt, idx, src, axis=0):
    return tgt.at[idx].add(src)

def _segment_sum(src, seg, n):
    return jax.ops.segment_sum(src, seg, n)
kernel_name = 'mk_seq_preln_d1_jaxref_r4_89ed1e'

def setup_inputs(seed: int=0):
    np.random.seed(seed)
    _w = jnp.asarray

    def _L0_attn_setup():
        import jax, jax.numpy as jnp
        import numpy as np
        ALPHA = 1.2
        A = 1.0
        BANDWIDTH = 1.0
        D_INTRINSIC = 2
        SPHERE_RADIUS = 1.0
        NUM_HEADS = 16
        HIDDEN = 256
        HEAD_DIM = HIDDEN // NUM_HEADS
        EPS = 1e-07

        def _l2norm(t):
            n = jnp.sqrt(jnp.sum(t * t, axis=-1, keepdims=True))
            return t / jnp.maximum(n, 1e-12)
        key = jax.random.key(seed)
        k1, k2, k3, k4, k5 = jax.random.split(key, 5)
        B, S = (2, 512)
        scale = 0.02
        return {'x': jax.random.normal(k1, (B, S, HIDDEN), dtype=jnp.float32), 'w_qkv': jax.random.normal(k2, (3 * HIDDEN, HIDDEN), dtype=jnp.float32) * scale, 'b_qkv': jnp.zeros((3 * HIDDEN,), dtype=jnp.float32), 'w_out': jax.random.normal(k3, (HIDDEN, HIDDEN), dtype=jnp.float32) * scale, 'b_out': jnp.zeros((HIDDEN,), dtype=jnp.float32)}
    _L0_attn_in = _L0_attn_setup()

    def _L0_ffn_setup():
        import jax, jax.numpy as jnp
        import numpy as np
        TOP_K = 2
        key = jax.random.key(seed)
        ks = jax.random.split(key, 8)
        B, S, D = (2, 512, 256)
        N_r, N_s = (16, 2)
        u = jax.random.normal(ks[0], (B, S, D), dtype=jnp.float32)
        centroids = jax.random.normal(ks[1], (N_r, D), dtype=jnp.float32)
        expert_biases = jnp.zeros((N_r,), dtype=jnp.float32)
        Wr = jax.random.normal(ks[2], (N_r, D, D), dtype=jnp.float32) * (1.0 / np.sqrt(D))
        br = jax.random.normal(ks[3], (N_r, D), dtype=jnp.float32) * 0.01
        Ws = jax.random.normal(ks[4], (N_s, D, D), dtype=jnp.float32) * (1.0 / np.sqrt(D))
        bs = jax.random.normal(ks[5], (N_s, D), dtype=jnp.float32) * 0.01
        return {'u': u, 'centroids': centroids, 'expert_biases': expert_biases, 'Wr': Wr, 'br': br, 'Ws': Ws, 'bs': bs}
    _L0_ffn_in = _L0_ffn_setup()
    _d = {'L0_attn_x': _L0_attn_in['x'], 'L0_attn_w_qkv': _L0_attn_in['w_qkv'], 'L0_attn_b_qkv': _L0_attn_in['b_qkv'], 'L0_attn_w_out': _L0_attn_in['w_out'], 'L0_attn_b_out': _L0_attn_in['b_out'], 'L0_ffn_centroids': _L0_ffn_in['centroids'], 'L0_ffn_expert_biases': _L0_ffn_in['expert_biases'], 'L0_ffn_Wr': _L0_ffn_in['Wr'], 'L0_ffn_br': _L0_ffn_in['br'], 'L0_ffn_Ws': _L0_ffn_in['Ws'], 'L0_ffn_bs': _L0_ffn_in['bs']}
    _x0 = _d['L0_attn_x']
    _d['L0_attn_x'] = jax.random.normal(jax.random.fold_in(jax.random.key(seed), 1), (2, 2048, 256), dtype=_x0.dtype)
    del _x0
    return _d

def reference(L0_attn_x, L0_attn_w_qkv, L0_attn_b_qkv, L0_attn_w_out, L0_attn_b_out, L0_ffn_centroids, L0_ffn_expert_biases, L0_ffn_Wr, L0_ffn_br, L0_ffn_Ws, L0_ffn_bs):

    def _L0_attn_ref(x, w_qkv, b_qkv, w_out, b_out):
        import jax, jax.numpy as jnp
        import numpy as np
        ALPHA = 1.2
        A = 1.0
        BANDWIDTH = 1.0
        D_INTRINSIC = 2
        SPHERE_RADIUS = 1.0
        NUM_HEADS = 16
        HIDDEN = 256
        HEAD_DIM = HIDDEN // NUM_HEADS
        EPS = 1e-07

        def _l2norm(t):
            n = jnp.sqrt(jnp.sum(t * t, axis=-1, keepdims=True))
            return t / jnp.maximum(n, 1e-12)
        B, S, H = x.shape
        qkv = x @ w_qkv.T + b_qkv
        q, k, v = jnp.split(qkv, 3, axis=-1)
        to_heads = lambda t: t.reshape(B, S, NUM_HEADS, HEAD_DIM).transpose(0, 2, 1, 3)
        q = _l2norm(to_heads(q))
        k = _l2norm(to_heads(k))
        v = to_heads(v)
        cos = jnp.einsum('bhsd,bhtd->bhst', q, k)
        g_dist = jnp.arccos(jnp.clip(cos, -1.0 + EPS, 1.0 - EPS)) * SPHERE_RADIUS
        attn_score = (1.0 + g_dist / BANDWIDTH ** 0.5) ** (-D_INTRINSIC - ALPHA)
        n_r = jnp.sum(attn_score, axis=-1)
        n_c = jnp.sum(attn_score, axis=-2)
        k_tilde = (n_r ** (-A))[..., :, None] * attn_score * (n_c ** (-A))[..., None, :]
        probs = k_tilde / jnp.maximum(jnp.sum(k_tilde, axis=-1, keepdims=True), 1e-12)
        out = jnp.einsum('bhst,bhtd->bhsd', probs, v)
        out = out.transpose(0, 2, 1, 3).reshape(B, S, H)
        return out @ w_out.T + b_out

    def _L0_ffn_ref(u, centroids, expert_biases, Wr, br, Ws, bs):
        import jax, jax.numpy as jnp
        import numpy as np
        TOP_K = 2
        N_r = centroids.shape[0]
        N_s = Ws.shape[0]
        raw_scores = jnp.einsum('bsd,ed->bse', u, centroids)
        s = jax.nn.softmax(raw_scores + expert_biases, axis=-1)
        topk_vals, topk_idx = jax.lax.top_k(s, TOP_K)
        g_topk = jnp.sum(jax.nn.one_hot(topk_idx, N_r, dtype=s.dtype) * topk_vals[..., None], axis=-2)
        xe = jnp.einsum('bsd,eod->bseo', u, Wr) + br
        routed = jnp.einsum('bse,bseo->bso', g_topk, xe)
        shared = (jnp.einsum('bsd,eod->bso', u, Ws) + jnp.sum(bs, axis=0)) / N_s
        return u + routed + shared
    x = L0_attn_x
    x = x + _L0_attn_ref(_layernorm(x, axis=-1), L0_attn_w_qkv, L0_attn_b_qkv, L0_attn_w_out, L0_attn_b_out)
    x = x + _L0_ffn_ref(_layernorm(x, axis=-1), L0_ffn_centroids, L0_ffn_expert_biases, L0_ffn_Wr, L0_ffn_br, L0_ffn_Ws, L0_ffn_bs)
    return x

_drawn_inputs = setup_inputs


def setup_inputs(seed=0):
    import zlib

    import numpy as np

    out = dict(_drawn_inputs(seed))
    spreads = {'L0_attn_b_qkv': (0.0, 0.1),
     'L0_attn_b_out': (0.0, 0.1),
     'L0_ffn_expert_biases': (0.0, 0.8)}
    factors = {'L0_attn_w_qkv': 8.0, 'L0_ffn_br': 8.0, 'L0_ffn_bs': 8.0}
    for name, (base, spread) in spreads.items():
        noise = np.random.default_rng([zlib.crc32(name.encode()), seed]).standard_normal(out[name].shape)
        drawn = base * np.exp(spread * noise) if base else spread * noise
        out[name] = jnp.asarray(drawn.astype(out[name].dtype))
    for name, factor in factors.items():
        out[name] = (out[name] * factor).astype(out[name].dtype)
    return out
```

```python
import concourse.bass as bass
from concourse import mybir
from contextlib import ExitStack


def pre_ln_arccos_attention_moe_kernel(nc, x, w_qkv, b_qkv, w_out, b_out, centroids, expert_biases,
                                       Wr, br, Ws, bs, out):
    fp32 = mybir.dt.float32
    bf16 = mybir.dt.bfloat16
    ALU = mybir.AluOpType
    ACT = mybir.ActivationFunctionType
    AX = mybir.AxisListType

    B, S, D = x.shape
    P = 128
    HD = 16
    H = D // HD
    NH = B * H
    KT = S // P
    BT = KT // 2
    NB = 2 * NH
    KC = D // P
    NR = Wr.shape[0]
    NS = Ws.shape[0]
    G = 4
    NG = B * S // (G * P)
    GPB = NG // B
    GT = G * P
    PI = 3.141592653589793
    CLIP = 1.0 - 1e-7
    POWER = -2.0 - 1.2
    LN_EPS = 1e-5
    TINY = 1e-12

    x_rows = x.rearrange("b s d -> (b s) d")
    out_rows = out.rearrange("b s d -> (b s) d")
    qk_parts = nc.dram_tensor("qk_parts", (2, 3, NH, HD, S), bf16, kind="Internal").ap()
    head_out = nc.dram_tensor("head_out", (NH, 4, 32, 512), fp32, kind="Internal").ap()
    row_scale = nc.dram_tensor("row_scale", (NH, 4, 512), fp32, kind="Internal").ap()

    ctx = ExitStack()
    with ctx:
        def sb(name, shape, dt):
            return ctx.enter_context(nc.sbuf_tensor(name, shape, dt))

        def pb(name, shape, dt):
            return ctx.enter_context(nc.psum_tensor(name, shape, dt))

        def sem(name):
            return ctx.enter_context(nc.semaphore(name))

        X = sb("X", [P, 2, BT, S], fp32)
        V = sb("V", [P, NH, KT, HD], fp32)
        cosc = sb("cosc", [P, 2, S], fp32)
        stacks = sb("stacks", [P, 2, 2, S], bf16)
        vp = sb("vp", [P, 4, 32], fp32)
        ncol = sb("ncol", [P, BT], fp32)
        evac = sb("evac", [P, 2, 512], fp32)
        ident = sb("ident", [P, P], fp32)
        identb = sb("identb", [P, P], bf16)
        ones = sb("ones", [1, P], fp32)
        consts = sb("consts", [P, 4], fp32)
        one_c, theta_c, eps_c = consts[:, 0:1], consts[:, 1:2], consts[:, 2:3]

        flat = X[:, :, :, :].rearrange("p a b c -> p (a b c)")
        at = [0]

        def carve(dims, dt=fp32, parts=P):
            n = 1
            for d in dims:
                n *= d
            words = n if dt == fp32 else n // 2
            v = flat[0:parts, at[0]:at[0] + words]
            at[0] += words
            assert at[0] <= 2 * BT * S
            if dt != fp32:
                v = v.bitcast(dt)
            if len(dims) == 1:
                return v
            names = "abcd"[:len(dims)]
            return v.rearrange("p (" + " ".join(names) + ") -> p " + " ".join(names),
                               **{m: d for m, d in zip(names, dims)})

        psum = pb("psum", [P, 8, 512], fp32)
        banks = [psum[:, i, :] for i in range(8)]

        w_nat = carve([6, D])
        w_t = carve([KC, 3 * D])
        bq_row = carve([3 * D], parts=1)
        xin = [carve([G, D]) for _ in range(2)]
        xn = [carve([G, D]) for _ in range(2)]
        xn_t = [carve([KC, GT]) for _ in range(2)]
        sq = [carve([2 * D]) for _ in range(2)]
        qn = carve([G, 2 * D])
        rest = carve([G, 2 * D])
        parts = carve([G, 3, 2 * D], bf16)
        parts_t = [carve([12, GT], bf16) for _ in range(2)]
        stats = carve([G, 6])
        mv = carve([G, 2])
        sd = carve([G])
        rstd = carve([G])
        ssum = [carve([2 * H]) for _ in range(2)]
        norm = [carve([2 * H]) for _ in range(2)]
        rnorm = [carve([2 * H]) for _ in range(2)]
        ps_xt = banks[0:2]
        ps_qk = banks[2:4]
        ps_v = [banks[4][:, 0:D], banks[5][:, 0:D]]
        ps_pt = [banks[6][:, :].bitcast(bf16), banks[7][:, :].bitcast(bf16)]

        made = sem("made")
        w_in = sem("w_in")
        w_ps = sem("w_ps")
        w_sb = sem("w_sb")
        x_in = [sem(f"x_in{m}") for m in range(2)]
        x_used = sem("x_used")
        var_ok = sem("var_ok")
        sd_ok = sem("sd_ok")
        xn_ok = sem("xn_ok")
        xt_ps = sem("xt_ps")
        xt_ok = sem("xt_ok")
        qk_ps = sem("qk_ps")
        sq_ok = sem("sq_ok")
        ss_ok = sem("ss_ok")
        norm_ok = sem("norm_ok")
        v_ok = sem("v_ok")
        qn_ok = sem("qn_ok")
        hi_ok = sem("hi_ok")
        rest_ok = sem("rest_ok")
        mid_ok = sem("mid_ok")
        low_ok = sem("low_ok")
        pt0_ps = sem("pt0_ps")
        pt1_ps = sem("pt1_ps")
        pt0_ok = sem("pt0_ok")
        pt1_ok = sem("pt1_ok")
        parts_out = sem("parts_out")
        dve_step = sem("dve_step")
        un_step = sem("un_step")

        def wait(engine, semaphore, value):
            if not isinstance(value, int) or value > 0:
                engine.wait_ge(semaphore, value)

        held = sem("held")

        def hold(engine, semaphore, value):
            engine.wait_ge(semaphore, value)
            engine.sem_inc(held, 1)

        def ps_qk_of(m, j):
            return ps_qk[j % 2][:, :]

        LOOP1 = NG // 2 - 1

        with nc.Block() as block:
            @block.gpsimd
            def _(pool):
                nc.gpsimd.memset(ident[:, :], 0.0).then_inc(made, 1)
                nc.gpsimd.memset(identb[:, :], 0.0).then_inc(made, 1)
                nc.gpsimd.memset(ones[:, :], 1.0).then_inc(made, 1)
                nc.gpsimd.memset(one_c, 1.0).then_inc(made, 1)
                nc.gpsimd.memset(theta_c, 1.0 + PI / 2).then_inc(made, 1)
                nc.gpsimd.memset(eps_c, LN_EPS).then_inc(made, 1)
                nc.gpsimd.memset(vp[:, :, :], 0.0).then_inc(made, 1)
                pool.wait_ge(made, 7)
                for m in (ident, identb):
                    nc.gpsimd.affine_select(out=m[:, :], in_=m[:, :], compare_op=ALU.not_equal, fill=1.0,
                                            base=0, pattern=[[-1, P]], channel_multiplier=1).then_inc(made, 1)
                nc.gpsimd.memset(vp[:, :, 17:18], 1.0).then_inc(made, 1)

            @block.sync
            def _(sp):
                sp.dma_start(w_nat, w_qkv.rearrange("(c p) d -> p c d", p=P)).then_inc(w_in, 16)
                sp.dma_start(bq_row, b_qkv.rearrange("(a n) -> a n", a=1)).then_inc(w_in, 16)

                def load(g, m):
                    sp.dma_start(xin[m], x_rows[bass.ds(g * GT, GT), :].rearrange("(j p) d -> p j d", p=P)
                                 ).then_inc(x_in[m], 16)

                def step(k, m, last):
                    if not last:
                        hold(sp, x_used, (2 * k + m) * G + G)
                        load(2 * k + m + 2, m)
                    hold(sp, pt0_ok, (2 * k + m) * G + G)
                    hold(sp, pt1_ok, (2 * k + m) * G + G)
                    for c in range(4):
                        for p in range(3):
                            dst = qk_parts[c // 2, p, bass.ds((k // (GPB // 2)) * H + c % 2 * 8, 8), :,
                                           bass.ds((k % (GPB // 2)) * 2 * GT + m * GT, GT)]
                            sp.dma_start(dst, parts_t[m][:, p * 4 + c, :]).then_inc(parts_out, 16)
                    hold(sp, parts_out, (2 * k + m) * 192 + 192)

                load(0, 0)
                load(1, 1)
                step(0, 0, False)
                step(0, 1, False)
                with sp.Fori(1, LOOP1) as k:
                    step(k, 0, False)
                    step(k, 1, False)
                step(LOOP1, 0, True)
                step(LOOP1, 1, True)

            @block.scalar
            def _(act):
                for c in range(6):
                    act.wait_ge(w_ps, c + 1)
                    nc.scalar.activation(w_t[:, :, c * P:(c + 1) * P],
                                         banks[c % 2][:, 0:KC * P].rearrange("p (k n) -> p k n", k=KC),
                                         ACT.Copy).then_inc(w_sb, 1)

                def standard(k, m):
                    g = 2 * k + m
                    act.wait_ge(var_ok, g * G + G)
                    nc.scalar.activation(sd, mv[:, :, 1], ACT.Sqrt, bias=eps_c).then_inc(sd_ok, 1)
                    for c in range(KC):
                        act.wait_ge(xt_ps, g * KC + c + 1)
                        if c == 0:
                            wait(act, qk_ps, (g - 1) * G)
                        nc.scalar.activation(xn_t[m % 2][:, c, :], ps_xt[c][:, :], ACT.Copy).then_inc(xt_ok, 1)

                def squares(k, m, j):
                    t = (2 * k + m) * G + j
                    act.wait_ge(qk_ps, t + 1)
                    wait(act, ss_ok, t - 1)
                    nc.scalar.activation(sq[j % 2], ps_qk_of(m, j), ACT.Square).then_inc(sq_ok, 1)
                    nc.scalar.activation(V[:, bass.ds((k // (GPB // 2)) * H, H),
                                           bass.ds((k % (GPB // 2)) * 2 * G + m * G + j, 1), :],
                                         ps_v[j % 2].rearrange(
                                             "p (h o d) -> p h o d", h=H, o=1),
                                         ACT.Copy).then_inc(v_ok, 1)

                def norms(k, m, j):
                    act.wait_ge(ss_ok, (2 * k + m) * G + j + 1)
                    nc.scalar.activation(norm[j % 2], ssum[j % 2], ACT.Sqrt).then_inc(norm_ok, 1)

                def step(k, m, last):
                    g = 2 * k + m
                    squares(k, m, 0)
                    for j in range(1, G):
                        squares(k, m, j)
                        norms(k, m, j - 1)
                    norms(k, m, G - 1)
                    if not last:
                        standard(k, m + 1)
                    act.wait_ge(qn_ok, g * G + G)
                    wait(act, pt1_ps, g * G)
                    for a in range(2):
                        nc.scalar.activation(parts[:, 2 * a:2 * a + 2, 0, :], qn[:, 2 * a:2 * a + 2, :],
                                             ACT.Copy).then_inc(hi_ok, 1)
                    for a in range(2):
                        act.wait_ge(rest_ok, g * 2 + a + 1)
                        nc.scalar.activation(parts[:, 2 * a:2 * a + 2, 1, :], rest[:, 2 * a:2 * a + 2, :],
                                             ACT.Copy).then_inc(mid_ok, 1)
                    for j in range(G):
                        act.wait_ge(pt0_ps, g * G + j + 1)
                        if j == 0:
                            wait(act, parts_out, (g - 1) * 192)
                        nc.scalar.activation(parts_t[m][:, 0:8, j * P:(j + 1) * P],
                                             ps_pt[0].rearrange("p (c n) -> p c n", c=8),
                                             ACT.Copy).then_inc(pt0_ok, 1)

                standard(0, 0)
                step(0, 0, False)
                step(0, 1, False)
                with act.Fori(1, LOOP1) as k:
                    step(k, 0, False)
                    step(k, 1, False)
                step(LOOP1, 0, False)
                step(LOOP1, 1, True)

            @block.vector
            def _(dve):
                def centre(k, m):
                    g = 2 * k + m
                    dve.wait_ge(x_in[m % 2], (k + m // 2) * 16 + 16)
                    for j in range(G):
                        nc.vector.bn_stats(stats[:, j, :], xin[m % 2][:, j, :]).then_inc(dve_step, 1)
                    hold(dve, dve_step, g * (G + 1) + G)
                    for j in range(G):
                        nc.vector.bn_aggr(mv[:, j, :], stats[:, j, :]).then_inc(var_ok, 1)
                    dve.wait_ge(sd_ok, g + 1)
                    nc.vector.reciprocal(rstd, sd).then_inc(dve_step, 1)
                    dve.wait_ge(dve_step, g * (G + 1) + G + 1)
                    for j in range(G):
                        if j == 0:
                            wait(dve, xt_ps, (g - 1) * KC)
                        nc.vector.tensor_scalar(xn[m % 2][:, j, :], xin[m % 2][:, j, :], mv[:, j, 0:1],
                                                rstd[:, j:j + 1], ALU.subtract, ALU.mult).then_inc(x_used, 1)

                def sums(k, m, j):
                    t = (2 * k + m) * G + j
                    dve.wait_ge(sq_ok, t + 1)
                    wait(dve, norm_ok, t - 1)
                    nc.vector.reduce_sum(ssum[j % 2], sq[j % 2].rearrange("p (h d) -> p h d", d=HD),
                                         AX.X).then_inc(ss_ok, 1)

                def unit(k, m, j):
                    t = (2 * k + m) * G + j
                    dve.wait_ge(norm_ok, t + 1)
                    nc.vector.tensor_scalar_max(norm[j % 2], norm[j % 2], TINY).then_inc(un_step, 1)
                    dve.wait_ge(un_step, t * 2 + 1)
                    nc.vector.reciprocal(rnorm[j % 2], norm[j % 2]).then_inc(un_step, 1)
                    dve.wait_ge(un_step, t * 2 + 2)
                    if j == 0:
                        wait(dve, hi_ok, (2 * k + m) * 2)
                    nc.vector.tensor_tensor(qn[:, j, :].rearrange("p (h d) -> p h d", d=HD),
                                            ps_qk_of(m, j).rearrange("p (h d) -> p h d", d=HD),
                                            rnorm[j % 2].unsqueeze(2).broadcast_to([P, 2 * H, HD]),
                                            ALU.mult).then_inc(qn_ok, 1)

                def step(k, m, last):
                    g = 2 * k + m
                    sums(k, m, 0)
                    for j in range(1, G):
                        sums(k, m, j)
                        unit(k, m, j - 1)
                    unit(k, m, G - 1)
                    if not last:
                        centre(k, m + 1)
                    for a in range(2):
                        dve.wait_ge(hi_ok, g * 2 + a + 1)
                        wait(dve, low_ok, g * 2)
                        nc.vector.tensor_tensor(rest[:, 2 * a:2 * a + 2, :], qn[:, 2 * a:2 * a + 2, :],
                                                parts[:, 2 * a:2 * a + 2, 0, :], ALU.subtract).then_inc(rest_ok, 1)
                    for a in range(2):
                        dve.wait_ge(mid_ok, g * 2 + a + 1)
                        nc.vector.tensor_tensor(parts[:, 2 * a:2 * a + 2, 2, :], rest[:, 2 * a:2 * a + 2, :],
                                                parts[:, 2 * a:2 * a + 2, 1, :], ALU.subtract).then_inc(low_ok, 1)
                    for j in range(G):
                        dve.wait_ge(pt1_ps, g * G + j + 1)
                        if j == 0:
                            wait(dve, parts_out, (g - 1) * 192)
                        nc.vector.tensor_copy(parts_t[m][:, 8:12, j * P:(j + 1) * P],
                                              ps_pt[1][:, 0:4 * P].rearrange("p (c n) -> p c n", c=4)
                                              ).then_inc(pt1_ok, 1)

                centre(0, 0)
                step(0, 0, False)
                step(0, 1, False)
                with dve.Fori(1, LOOP1) as k:
                    step(k, 0, False)
                    step(k, 1, False)
                step(LOOP1, 0, False)
                step(LOOP1, 1, True)

            @block.tensor
            def _(pe):
                pe.wait_ge(made, 10)
                pe.wait_ge(w_in, 32)
                for c in range(6):
                    if c >= 2:
                        pe.wait_ge(w_sb, c - 1)
                    for kc in range(KC):
                        last = nc.tensor.transpose(banks[c % 2][:, kc * P:(kc + 1) * P],
                                                   w_nat[:, c, kc * P:(kc + 1) * P], ident[:, :])
                    last.then_inc(w_ps, 1)
                pe.wait_ge(w_sb, 6)

                def rows_t(k, m):
                    g = 2 * k + m
                    pe.wait_ge(x_used, g * G + G)
                    wait(pe, xt_ok, g * KC)
                    for c in range(KC):
                        for j in range(G):
                            last = nc.tensor.transpose(ps_xt[c][:, j * P:(j + 1) * P],
                                                       xn[m % 2][:, j, c * P:(c + 1) * P], ident[:, :])
                        last.then_inc(xt_ps, 1)

                def project(k, m, j):
                    t = (2 * k + m) * G + j
                    wait(pe, qn_ok, t - 1)
                    wait(pe, v_ok, t - 1)
                    for c in range(KC):
                        nc.tensor.matmul(ps_qk_of(m, j), xn_t[m][:, c, j * P:(j + 1) * P],
                                         w_t[:, c, 0:2 * D], start=(c == 0), stop=False)
                    nc.tensor.matmul(ps_qk_of(m, j), ones[0:1, :], bq_row[0:1, 0:2 * D], start=False, stop=True)
                    pv = ps_v[j % 2]
                    for c in range(KC):
                        nc.tensor.matmul(pv, xn_t[m][:, c, j * P:(j + 1) * P],
                                         w_t[:, c, 2 * D:3 * D], start=(c == 0), stop=False)
                    nc.tensor.matmul(pv, ones[0:1, :], bq_row[0:1, 2 * D:3 * D],
                                     start=False, stop=True).then_inc(qk_ps, 1)

                def step(k, m, last):
                    g = 2 * k + m
                    pe.wait_ge(xt_ok, g * KC + KC)
                    for j in range(G):
                        project(k, m, j)
                    if not last:
                        rows_t(k, m + 1)
                    for j in range(G):
                        if j % 2 == 0:
                            pe.wait_ge(low_ok, g * 2 + j // 2 + 1)
                        t = g * G + j
                        for half, (ok, ps) in enumerate(((pt0_ok, pt0_ps), (pt1_ok, pt1_ps))):
                            wait(pe, ok, t)
                            for b in range(8 * half, 8 + 4 * half):
                                mm = nc.tensor.transpose(ps_pt[half][:, (b - 8 * half) * P:(b - 8 * half + 1) * P],
                                                         parts[:, j, b // 4, b % 4 * P:(b % 4 + 1) * P],
                                                         identb[:, :])
                            mm.then_inc(ps, 1)

                rows_t(0, 0)
                step(0, 0, False)
                step(0, 1, False)
                with pe.Fori(1, LOOP1) as k:
                    step(k, 0, False)
                    step(k, 1, False)
                step(LOOP1, 0, False)
                step(LOOP1, 1, True)


        ps_sum = banks[0:2]
        ps_clip = [psum[:, 2:4, :], psum[:, 4:6, :]]
        ps_mult = banks[6:8]

        stack_in = sem("stack_in")
        clip_ps = sem("clip_ps")
        clip_ok = sem("clip_ok")
        square_ok = sem("square_ok")
        log_ok = sem("log_ok")
        recip_ok = sem("recip_ok")
        mult_ps = sem("mult_ps")
        mult_ok = sem("mult_ok")
        atan_ok = sem("atan_ok")
        log2_ok = sem("log2_ok")
        score_ok = sem("score_ok")
        nc_ok = sem("nc_ok")
        vp_ok = sem("vp_ok")
        sum_ps = sem("sum_ps")
        sum_ok = sem("sum_ok")
        head_stored = [sem(f"head_stored{h}") for h in range(2)]
        LOADS = 11 * 16
        LAST = NB // 4 - 1

        def periods(engine, emit):
            for m in range(4):
                emit(0, m)
            with engine.Fori(1, LAST) as k:
                for m in range(4):
                    emit(k, m)
            for m in range(4):
                emit(LAST, m)

        def has(k, m):
            return not (isinstance(k, int) and 4 * k + m >= NB)

        with nc.Block() as block:
            @block.sync
            def _(sp):
                def load(k, h):
                    head, buf = 2 * k + h, h % 2
                    row = 0
                    for part, times in ((0, 3), (1, 3), (2, 2)):
                        for _ in range(times):
                            sp.dma_start(stacks[row:row + HD, 0, buf, :],
                                         qk_parts[0, part, bass.ds(head, 1), :, :].rearrange("o d s -> (o d) s")
                                         ).then_inc(stack_in, 16)
                            row += HD
                    for row, n in ((0, 3), (3, 3), (6, 2)):
                        sp.dma_start(stacks[row * HD:(row + n) * HD, 1, buf, :],
                                     qk_parts[1, 0:n, bass.ds(head, 1), :, :].rearrange("p o d s -> (p o) d s")
                                     ).then_inc(stack_in, 16)

                def emit(k, m):
                    n = 4 * k + m
                    if m % 2 == 0:
                        if has(k, m + 4):
                            hold(sp, mult_ok, (n + 2) * 4 * BT)
                            load(k, m // 2 + 2)
                    else:
                        head = 2 * k + m // 2
                        hold(sp, sum_ok, head + 1)
                        sp.dma_start(head_out[bass.ds(head, 1)].rearrange("o j r s -> (o j r) s"),
                                     evac[:, m // 2, :]).then_inc(head_stored[m // 2], 16)

                load(0, 0)
                load(0, 1)
                periods(sp, emit)
                for h in range(2):
                    sp.wait_ge(head_stored[h], NH // 2 * 16)

            @block.tensor
            def _(pe):
                def cosines(dst, m, i, q0, n):
                    buf = m // 2 % 2
                    keys = (m % 2 * BT + i) * P
                    return nc.tensor.matmul(dst, stacks[:, 1, buf, keys:keys + P],
                                            stacks[:, 0, buf, q0:q0 + n], start=True, stop=True)

                def clip(k, m, i):
                    for half in range(2):
                        wait(pe, clip_ok, ((4 * k + m) * BT + i) * 2 + half - 1)
                        for j in range(2):
                            mm = cosines(ps_clip[half][:, j, :], m, i, half * 1024 + j * 512, 512)
                        mm.then_inc(clip_ps, 1)

                def mult(k, m, i):
                    for j in range(4):
                        wait(pe, mult_ok, ((4 * k + m) * BT + i) * 4 + j - 1)
                        cosines(ps_mult[j % 2][:, :], m, i, j * 512, 512).then_inc(mult_ps, 1)

                def add(k, m, i):
                    t = (4 * k + m) * BT + i
                    pe.wait_ge(vp_ok, t + 1)
                    if m % 2 == 0 and i == 0:
                        wait(pe, sum_ok, 2 * k + m // 2 - 1)
                    for j in range(4):
                        mm = nc.tensor.matmul(ps_sum[m // 2][32 * j:32 * j + 32, :], vp[:, i % 4, :],
                                              X[:, m % 2, i, j * 512:(j + 1) * 512],
                                              start=(m % 2 == 0 and i == 0), stop=(m % 2 == 1 and i == BT - 1),
                                              tile_position=(0, 32 * j))
                    mm.then_inc(sum_ps, 1)

                def emit(k, m):
                    if m % 2 == 0 and has(k, m + 2):
                        pe.wait_ge(stack_in, (2 * k + m // 2 + 2) * LOADS)
                    for i in range(BT // 2):
                        if has(k, m + 2):
                            clip(k, m + 2, i)
                        add(k, m, 2 * i)
                        add(k, m, 2 * i + 1)
                    for i in range(BT // 2):
                        if has(k, m + 2):
                            clip(k, m + 2, BT // 2 + i)
                        if has(k, m + 1):
                            mult(k, m + 1, 2 * i)
                            mult(k, m + 1, 2 * i + 1)

                pe.wait_ge(stack_in, 2 * LOADS)
                for i in range(BT):
                    clip(0, 0, i)
                for i in range(BT):
                    clip(0, 1, i)
                    mult(0, 0, i)
                periods(pe, emit)

            @block.vector
            def _(dve):
                def clip(k, m, i):
                    t = (4 * k + m) * BT + i
                    wait(dve, square_ok, t - 1)
                    for half in range(2):
                        dve.wait_ge(clip_ps, t * 2 + half + 1)
                        nc.vector.tensor_scalar(cosc[:, i % 2, half * 1024:(half + 1) * 1024].rearrange(
                                                    "p (b n) -> p b n", b=2), ps_clip[half], -CLIP, CLIP,
                                                ALU.max, ALU.min).then_inc(clip_ok, 1)

                def mult(k, m, i):
                    t = (4 * k + m) * BT + i
                    dve.wait_ge(recip_ok, (4 * k + m) * (BT // 2) + i // 2 + 1)
                    for j in range(4):
                        dve.wait_ge(mult_ps, t * 4 + j + 1)
                        part = X[:, m % 2, i, j * 512:(j + 1) * 512]
                        nc.vector.tensor_tensor(part, ps_mult[j % 2][:, :], part, ALU.mult).then_inc(mult_ok, 1)

                def values(k, m, i):
                    t = (4 * k + m) * BT + i
                    dve.wait_ge(score_ok, t + 1)
                    wait(dve, sum_ps, t - 3)
                    nc.vector.reciprocal(vp[:, i % 4, HD:HD + 1], ncol[:, i:i + 1]).then_inc(nc_ok, 1)
                    dve.wait_ge(nc_ok, t + 1)
                    nc.vector.tensor_scalar(vp[:, i % 4, 0:HD],
                                            V[:, bass.ds(2 * k + m // 2, 1), m % 2 * BT + i, :].rearrange(
                                                "p o d -> p (o d)"),
                                            vp[:, i % 4, HD:HD + 1], None, ALU.mult).then_inc(vp_ok, 1)

                def emit(k, m):
                    for i in range(BT // 2):
                        values(k, m, 2 * i)
                        values(k, m, 2 * i + 1)
                        if has(k, m + 2):
                            clip(k, m + 2, i)
                    for i in range(BT // 2):
                        if has(k, m + 2):
                            clip(k, m + 2, BT // 2 + i)
                        if has(k, m + 1):
                            mult(k, m + 1, 2 * i)
                            mult(k, m + 1, 2 * i + 1)
                    if m % 2 == 1:
                        head = 2 * k + m // 2
                        dve.wait_ge(sum_ps, (head + 1) * KT)
                        wait(dve, head_stored[m // 2], k * 16)
                        nc.vector.tensor_copy(evac[:, m // 2, :], ps_sum[m // 2][:, :]).then_inc(sum_ok, 1)

                for i in range(BT):
                    clip(0, 0, i)
                for i in range(BT):
                    clip(0, 1, i)
                    mult(0, 0, i)
                periods(dve, emit)

            @block.gpsimd
            def _(pool):
                def square(k, m, i):
                    t = (4 * k + m) * BT + i
                    pool.wait_ge(clip_ok, t * 2 + 2)
                    wait(pool, sum_ps, t - 2 * BT + 1)
                    nc.gpsimd.tensor_tensor(X[:, m % 2, i, :], cosc[:, i % 2, :], cosc[:, i % 2, :],
                                            ALU.mult).then_inc(square_ok, 1)

                def emit(k, m):
                    if has(k, m + 2):
                        for i in range(BT):
                            square(k, m + 2, i)

                for m in range(2):
                    for i in range(BT):
                        square(0, m, i)
                periods(pool, emit)

            @block.scalar
            def _(act):
                def two(m, i):
                    return X[:, m % 2, 2 * i:2 * i + 2, :]

                def sines(k, m):
                    n = (4 * k + m) * (BT // 2)
                    for i in range(BT // 2):
                        act.wait_ge(square_ok, (n + i) * 2 + 2)
                        nc.scalar.activation(two(m, i), two(m, i), ACT.Ln, bias=one_c, scale=-1.0).then_inc(log_ok, 1)
                    for i in range(BT // 2):
                        act.wait_ge(log_ok, n + i + 1)
                        nc.scalar.activation(two(m, i), two(m, i), ACT.Sigmoid, scale=-0.5).then_inc(recip_ok, 1)
                    for i in range(BT // 2):
                        act.wait_ge(mult_ok, (n + i) * 8 + 8)
                        nc.scalar.activation(two(m, i), two(m, i), ACT.Arctan).then_inc(atan_ok, 1)

                def scores(k, m):
                    n = (4 * k + m) * (BT // 2)
                    for i in range(BT // 2):
                        act.wait_ge(atan_ok, n + i + 1)
                        nc.scalar.activation(two(m, i), two(m, i), ACT.Ln, bias=theta_c, scale=-2.0).then_inc(log2_ok, 1)
                    for i in range(BT):
                        act.wait_ge(log2_ok, n + i // 2 + 1)
                        nc.scalar.activation(X[:, m % 2, i, :], X[:, m % 2, i, :], ACT.Exp, scale=POWER,
                                             accum_out=ncol[:, i:i + 1]).then_inc(score_ok, 1)

                def emit(k, m):
                    scores(k, m)
                    if has(k, m + 1):
                        sines(k, m + 1)

                sines(0, 0)
                periods(act, emit)

        at[0] = 0
        NE = NR + 1
        NW = NE * D
        NX = NR + NS
        wr_nat = carve([NR, KC, D])
        ws_nat = carve([NS, KC, D])
        ws_sum = carve([KC, D])
        we_t = carve([KC, NW])
        wo_nat = carve([KC, D])
        wo_t = carve([KC, D])
        cen_nat = carve([D], parts=NR)
        cen_t = carve([KC, NR])
        bo_row = carve([D], parts=1)
        eb_row = carve([NR], parts=1)
        be_rows = carve([D], parts=NX)
        order = carve([NR])
        den = carve([512])
        nrow = carve([512])
        scl = carve([512])
        raw = carve([KC, GT])
        scale_b = carve([KC, GT])
        attn = carve([KC, GT])
        xres = carve([G, D])
        x1 = carve([D])
        u = carve([D])
        acc = [carve([D]) for _ in range(2)]
        u_t = [carve([KC, P]) for _ in range(2)]
        gate = [carve([NX]) for _ in range(2)]
        gate_t = [carve([P], parts=NX) for _ in range(2)]
        stat = carve([6])
        mean = carve([2])
        dev = carve([1])
        rdev = carve([1])
        top = carve([1])
        neg_top = carve([1])
        expd = carve([NR])
        esum = carve([1])
        resum = carve([1])
        prob = carve([NR])
        m1 = carve([1])
        t1 = carve([NR])
        w1 = carve([1])
        f1 = carve([NR])
        p2 = carve([NR])
        m2 = carve([1])
        t2 = carve([NR])
        w2 = carve([1])
        f2 = carve([NR])
        ps_e = banks[0:3]
        ps_y, ps_u, ps_l, ps_g = banks[3], banks[4], banks[5], banks[6]
        ps_l = ps_l[:, 0:NR]

        t_in = sem("t_in")
        t_sums = sem("t_sums")
        t_made = sem("t_made")
        t_ws = sem("t_ws")
        t_ps = sem("t_ps")
        t_sb = sem("t_sb")
        scale_ok = sem("scale_ok")
        scale_out = sem("scale_out")
        raw_in = sem("raw_in")
        xres_in = sem("xres_in")
        attn_ok = sem("attn_ok")
        y_ps = sem("y_ps")
        x1_ok = sem("x1_ok")
        var2_ok = sem("var2_ok")
        dev_ok = sem("dev_ok")
        u_ok = sem("u_ok")
        acc0_ok = sem("acc0_ok")
        u_ps = sem("u_ps")
        ut_ok = sem("ut_ok")
        l_ps = sem("l_ps")
        top_ok = sem("top_ok")
        exp_ok = sem("exp_ok")
        gate_ok = sem("gate_ok")
        g_ps = sem("g_ps")
        gt_ok = sem("gt_ok")
        e_ps = sem("e_ps")
        e_ok = sem("e_ok")
        rows_out = sem("rows_out")
        chain3 = sem("chain3")
        NT = NG * G

        def blocks(engine, emit):
            emit(0)
            with engine.Fori(1, NG - 1) as k:
                emit(k)
            emit(NG - 1)

        def final(k, j):
            return isinstance(k, int) and k == NG - 1 and j == G - 1

        with nc.Block() as block:
            @block.gpsimd
            def _(pool):
                for e in range(NR):
                    nc.gpsimd.memset(order[:, e:e + 1], float(NR - e)).then_inc(t_made, 1)
                for g in gate:
                    nc.gpsimd.memset(g[:, NR:NX], 1.0 / NS).then_inc(t_made, 1)

            @block.sync
            def _(sp):
                sp.dma_start(den, head_out[:, :, HD, :].rearrange("h j s -> (h j) s")).then_inc(t_sums, 16)
                sp.dma_start(nrow, head_out[:, :, HD + 1, :].rearrange("h j s -> (h j) s")).then_inc(t_sums, 16)
                sp.dma_start(ws_nat.rearrange("p e c d -> p (e c) d"),
                             Ws.rearrange("e (c p) d -> p (e c) d", p=P)).then_inc(t_ws, 16)
                sp.dma_start(wo_nat, w_out.rearrange("(c p) d -> p c d", p=P)).then_inc(t_in, 16)
                sp.dma_start(cen_nat, centroids).then_inc(t_in, 16)
                sp.dma_start(bo_row, b_out.rearrange("(a n) -> a n", a=1)).then_inc(t_in, 16)
                sp.dma_start(eb_row, expert_biases.rearrange("(a n) -> a n", a=1)).then_inc(t_in, 16)
                sp.dma_start(be_rows[0:NR, :], br).then_inc(t_in, 16)
                sp.dma_start(be_rows[NR:NX, :], bs).then_inc(t_in, 16)
                sp.dma_start(wr_nat.rearrange("p e c d -> p (e c) d"),
                             Wr.rearrange("e (c p) d -> p (e c) d", p=P)).then_inc(t_in, 16)
                sp.wait_ge(scale_ok, 1)
                sp.dma_start(row_scale.rearrange("h j s -> (h j) s"), scl).then_inc(scale_out, 16)
                sp.wait_ge(scale_out, 16)

                def load_raw(k):
                    for c in range(KC):
                        heads = bass.ds((k // GPB) * H + c * 8, 8)
                        sp.dma_start(raw[:, c, :], head_out[heads, bass.ds(k % GPB, 1), 0:HD, :].rearrange(
                            "h o r s -> (h o) r s")).then_inc(raw_in, 16)
                        sp.dma_start(scale_b[:, c, :], row_scale[heads, bass.ds(k % GPB, 1), :].broadcast_to(
                            [8, HD, 512])).then_inc(raw_in, 16)

                def load_x(k):
                    sp.dma_start(xres, x_rows[bass.ds(k * GT, GT), :].rearrange("(j p) d -> p j d", p=P)
                                 ).then_inc(xres_in, 16)

                def store(k, j):
                    hold(sp, e_ok, (k * G + j + 1) * NE)
                    sp.dma_start(out_rows[bass.ds((k * G + j) * P, P), :], acc[j % 2]).then_inc(rows_out, 16)
                    hold(sp, rows_out, (k * G + j + 1) * 16)

                def emit(k):
                    last = isinstance(k, int) and k == NG - 1
                    if not last:
                        hold(sp, attn_ok, k * KC + KC)
                        load_raw(k + 1)
                    for j in range(G):
                        store(k, j)
                        if j == G - 2 and not last:
                            hold(sp, x1_ok, (k + 1) * G)
                            load_x(k + 1)

                load_raw(0)
                load_x(0)
                blocks(sp, emit)

            @block.tensor
            def _(pe):
                n = 0
                pe.wait_ge(t_in, 7 * 16)
                pe.wait_ge(t_made, NR + 2)
                pe.wait_ge(chain3, 1)
                for e in range(NE):
                    if e >= 2:
                        pe.wait_ge(t_sb, e - 1)
                    for dc in range(KC):
                        for oc in range(KC):
                            nat = wr_nat[:, e, oc, dc * P:(dc + 1) * P] if e < NR else ws_sum[:, oc, dc * P:(dc + 1) * P]
                            mm = nc.tensor.transpose(ps_e[e % 2][:, (dc * KC + oc) * P:(dc * KC + oc + 1) * P],
                                                     nat, ident[:, :])
                    mm.then_inc(t_ps, 1)
                for dc in range(KC):
                    for oc in range(KC):
                        mm = nc.tensor.transpose(ps_y[:, (dc * KC + oc) * P:(dc * KC + oc + 1) * P],
                                                 wo_nat[:, oc, dc * P:(dc + 1) * P], ident[:, :])
                mm.then_inc(t_ps, 1)
                for dc in range(KC):
                    mm = nc.tensor.transpose(ps_u[:, dc * NR:(dc + 1) * NR], cen_nat[:, dc * P:(dc + 1) * P],
                                             ident[0:NR, 0:NR])
                mm.then_inc(t_ps, 1)
                pe.wait_ge(t_sb, NE + 2)

                def y(k, j):
                    t = k * G + j
                    if j == 0:
                        pe.wait_ge(attn_ok, k * KC + KC)
                    wait(pe, x1_ok, t)
                    for c in range(KC):
                        nc.tensor.matmul(ps_y[:, 0:D], attn[:, c, j * P:(j + 1) * P], wo_t[:, c, :],
                                         start=(c == 0), stop=False)
                    nc.tensor.matmul(ps_y[:, 0:D], ones[0:1, :], bo_row[0:1, :], start=False,
                                     stop=True).then_inc(y_ps, 1)

                def u_rows(k, j):
                    t = k * G + j
                    pe.wait_ge(u_ok, t + 1)
                    wait(pe, ut_ok, t)
                    for c in range(KC):
                        mm = nc.tensor.transpose(ps_u[:, c * P:(c + 1) * P], u[:, c * P:(c + 1) * P], ident[:, :])
                    mm.then_inc(u_ps, 1)

                def logits(k, j):
                    t = k * G + j
                    pe.wait_ge(ut_ok, t + 1)
                    wait(pe, exp_ok, t)
                    for c in range(KC):
                        nc.tensor.matmul(ps_l, u_t[j % 2][:, c, :], cen_t[:, c, :], start=(c == 0), stop=False)
                    nc.tensor.matmul(ps_l, ones[0:1, :], eb_row[0:1, :], start=False, stop=True).then_inc(l_ps, 1)

                def gates(k, j):
                    t = k * G + j
                    pe.wait_ge(gate_ok, t + 1)
                    wait(pe, gt_ok, t)
                    nc.tensor.transpose(ps_g[0:NX, 0:P], gate[j % 2], ident[:, :]).then_inc(g_ps, 1)

                def experts(k, j, c):
                    wait(pe, e_ok, (k * G + j) * NE + (-3, -1, 0, 2, 4, 6, 8, 10, 12)[c])
                    wide = 2 * D if c < NR // 2 else D
                    dst = ps_e[c % 3][:, 0:wide]
                    for kc in range(KC):
                        mm = nc.tensor.matmul(dst, u_t[j % 2][:, kc, :], we_t[:, kc, c * 2 * D:c * 2 * D + wide],
                                              start=(kc == 0), stop=(kc == KC - 1 and wide == 2 * D))
                    if wide == D:
                        pe.wait_ge(gt_ok, k * G + j + 1)
                        mm = nc.tensor.matmul(dst, gate_t[j % 2], be_rows, start=False, stop=True)
                    mm.then_inc(e_ps, 1)

                y(0, 0)
                u_rows(0, 0)
                logits(0, 0)
                gates(0, 0)

                def emit(k):
                    for j in range(G):
                        nk, nj = (k, j + 1) if j < G - 1 else (k + 1, 0)
                        more = not final(k, j)
                        if more:
                            y(nk, nj)
                        for c in range(3):
                            experts(k, j, c)
                        if more:
                            u_rows(nk, nj)
                        for c in range(3, 5):
                            experts(k, j, c)
                        if more:
                            logits(nk, nj)
                        for c in range(5, 9):
                            experts(k, j, c)
                        if more:
                            gates(nk, nj)

                blocks(pe, emit)

            @block.scalar
            def _(act):
                for e in range(0, NE, 2):
                    act.wait_ge(t_ps, e + 1)
                    if e:
                        act.wait_ge(t_sb, e)
                    nc.scalar.activation(we_t[:, :, e * D:(e + 1) * D],
                                         ps_e[e % 2][:, :].rearrange("p (k n) -> p k n", k=KC), ACT.Copy,
                                         scale=1.0 if e < NR else 1.0 / NS).then_inc(t_sb, 1)

                def sd3(k, j):
                    act.wait_ge(var2_ok, k * G + j + 1)
                    nc.scalar.activation(dev, mean[:, 1:2], ACT.Sqrt, bias=eps_c).then_inc(dev_ok, 1)

                def ut(k, j):
                    t = k * G + j
                    act.wait_ge(u_ps, t + 1)
                    wait(act, e_ps, (t - 1) * 9)
                    nc.scalar.activation(u_t[j % 2], ps_u[:, 0:D].rearrange("p (k n) -> p k n", k=KC),
                                         ACT.Copy).then_inc(ut_ok, 1)

                def exps(k, j):
                    act.wait_ge(top_ok, k * G + j + 1)
                    nc.scalar.activation(expd, ps_l, ACT.Exp, bias=neg_top, accum_out=esum).then_inc(exp_ok, 1)

                def gt(k, j):
                    act.wait_ge(g_ps, k * G + j + 1)
                    nc.scalar.activation(gate_t[j % 2], ps_g[0:NX, 0:P], ACT.Copy).then_inc(gt_ok, 1)

                def tile(k, j):
                    sd3(k, j)
                    ut(k, j)
                    exps(k, j)
                    gt(k, j)

                def emit(k):
                    for j in range(G):
                        if not final(k, j):
                            tile(*((k, j + 1) if j < G - 1 else (k + 1, 0)))

                tile(0, 0)
                blocks(act, emit)

            @block.vector
            def _(dve):
                count = [0]

                def link(ins):
                    count[0] = count[0] + 1
                    ins.then_inc(chain3, 1)
                    dve.wait_ge(chain3, count[0])

                dve.wait_ge(t_ws, 16)
                link(nc.vector.tensor_tensor(ws_sum, ws_nat[:, 0, :, :], ws_nat[:, 1, :, :], ALU.add))
                dve.wait_ge(t_sums, 32)
                link(nc.vector.reciprocal(nrow, nrow))
                link(nc.vector.tensor_tensor(den, den, nrow, ALU.mult))
                link(nc.vector.tensor_scalar_max(den, den, TINY))
                link(nc.vector.reciprocal(den, den))
                nc.vector.tensor_tensor(scl, den, nrow, ALU.mult).then_inc(scale_ok, 1)
                for e in range(1, NE, 2):
                    dve.wait_ge(t_ps, e + 1)
                    dve.wait_ge(t_sb, e)
                    nc.vector.tensor_copy(we_t[:, :, e * D:(e + 1) * D],
                                          ps_e[e % 2][:, :].rearrange("p (k n) -> p k n", k=KC)).then_inc(t_sb, 1)
                dve.wait_ge(t_ps, NE + 2)
                nc.vector.tensor_copy(wo_t, ps_y[:, :].rearrange("p (k n) -> p k n", k=KC)).then_inc(t_sb, 1)
                nc.vector.tensor_copy(cen_t, ps_u[:, 0:KC * NR].rearrange("p (k n) -> p k n", k=KC)
                                      ).then_inc(t_sb, 1)

                def scaled(k):
                    dve.wait_ge(raw_in, (k + 1) * 4 * 16)
                    wait(dve, y_ps, k * G)
                    for c in range(KC):
                        nc.vector.tensor_tensor(attn[:, c, :], raw[:, c, :], scale_b[:, c, :],
                                                ALU.mult).then_inc(attn_ok, 1)

                def residual(k, j):
                    t = k * G + j
                    if j == 0:
                        dve.wait_ge(xres_in, (k + 1) * 16)
                    dve.wait_ge(y_ps, t + 1)
                    nc.vector.tensor_tensor(x1, ps_y[:, 0:D], xres[:, j, :], ALU.add).then_inc(x1_ok, 1)
                    dve.wait_ge(x1_ok, t + 1)
                    link(nc.vector.bn_stats(stat, x1))
                    dve.sem_inc(held, 1)
                    nc.vector.bn_aggr(mean, stat).then_inc(var2_ok, 1)

                def centred(k, j):
                    t = k * G + j
                    dve.wait_ge(dev_ok, t + 1)
                    link(nc.vector.reciprocal(rdev, dev))
                    wait(dve, u_ps, t)
                    nc.vector.tensor_scalar(u, x1, mean[:, 0:1], rdev, ALU.subtract, ALU.mult).then_inc(u_ok, 1)
                    dve.wait_ge(u_ok, t + 1)
                    wait(dve, rows_out, (t - 1) * 16)
                    link(nc.vector.tensor_tensor(acc[j % 2], x1, u, ALU.add))

                def highest(k, j):
                    dve.wait_ge(l_ps, k * G + j + 1)
                    link(nc.vector.reduce_max(top, ps_l, AX.X))
                    nc.vector.tensor_scalar(neg_top, top, -1.0, None, ALU.mult).then_inc(top_ok, 1)

                def choose(k, j):
                    t = k * G + j
                    dve.wait_ge(exp_ok, t + 1)
                    link(nc.vector.reciprocal(resum, esum))
                    link(nc.vector.tensor_scalar(prob, expd, resum, None, ALU.mult))
                    link(nc.vector.reduce_max(m1, prob, AX.X))
                    link(nc.vector.scalar_tensor_tensor(t1, prob, m1, order, ALU.is_equal, ALU.mult))
                    link(nc.vector.reduce_max(w1, t1, AX.X))
                    link(nc.vector.tensor_scalar(f1, t1, w1, None, ALU.is_equal))
                    link(nc.vector.scalar_tensor_tensor(p2, f1, -2.0, prob, ALU.mult, ALU.add))
                    link(nc.vector.reduce_max(m2, p2, AX.X))
                    link(nc.vector.scalar_tensor_tensor(t2, p2, m2, order, ALU.is_equal, ALU.mult))
                    link(nc.vector.reduce_max(w2, t2, AX.X))
                    link(nc.vector.scalar_tensor_tensor(f2, t2, w2, f1, ALU.is_equal, ALU.add))
                    wait(dve, g_ps, t - 1)
                    nc.vector.tensor_tensor(gate[j % 2][:, 0:NR], prob, f2, ALU.mult).then_inc(gate_ok, 1)
                    dve.wait_ge(gate_ok, t + 1)

                def gather(k, j, c):
                    t = k * G + j
                    dve.wait_ge(e_ps, t * 9 + c + 1)
                    bank = ps_e[c % 3]
                    if c == NR // 2:
                        nc.vector.tensor_tensor(acc[j % 2], bank[:, 0:D], acc[j % 2], ALU.add).then_inc(e_ok, 1)
                        dve.wait_ge(e_ok, (t + 1) * NE)
                        return
                    for h in range(2):
                        e = 2 * c + h
                        nc.vector.scalar_tensor_tensor(acc[j % 2], bank[:, h * D:(h + 1) * D],
                                                       gate[j % 2][:, e:e + 1], acc[j % 2],
                                                       ALU.mult, ALU.add).then_inc(e_ok, 1)
                        dve.wait_ge(e_ok, t * NE + e + 1)

                scaled(0)
                residual(0, 0)
                centred(0, 0)
                highest(0, 0)
                choose(0, 0)
                start = count[0]
                per = [0]

                def emit(k):
                    if not isinstance(k, int) or k:
                        count[0] = start + k * per[0]
                    for j in range(G):
                        nk, nj = (k, j + 1) if j < G - 1 else (k + 1, 0)
                        more = not final(k, j)
                        if more:
                            if nj == 0:
                                scaled(nk)
                            residual(nk, nj)
                        gather(k, j, 0)
                        gather(k, j, 1)
                        if more:
                            centred(nk, nj)
                        gather(k, j, 2)
                        gather(k, j, 3)
                        gather(k, j, 4)
                        if more:
                            highest(nk, nj)
                        gather(k, j, 5)
                        if more:
                            choose(nk, nj)
                        for c in range(6, 9):
                            gather(k, j, c)
                    if isinstance(k, int) and k == 0:
                        per[0] = count[0] - start

                blocks(dve, emit)


_INS = ['L0_attn_x', 'L0_attn_w_qkv', 'L0_attn_b_qkv', 'L0_attn_w_out', 'L0_attn_b_out', 'L0_ffn_centroids',
        'L0_ffn_expert_biases', 'L0_ffn_Wr', 'L0_ffn_br', 'L0_ffn_Ws', 'L0_ffn_bs']
_OUTS = [((2, 2048, 256), 'float32')]


def kernel(**inputs):
    import numpy as _np
    import concourse.bacc as _bacc
    from concourse import mybir as _mybir
    from concourse.bass_utils import run_bass_kernel_spmd as _run

    nc = _bacc.Bacc("TRN2", target_bir_lowering=False, num_devices=1)
    arrays, args = {}, []
    for name in _INS:
        a = _np.ascontiguousarray(inputs[name])
        arrays[f"in_{name}_dram"] = a
        args.append(nc.dram_tensor(f"in_{name}_dram", a.shape, _mybir.dt.from_np(a.dtype), kind="ExternalInput").ap())
    for i, (shape, dtype) in enumerate(_OUTS):
        dt = _mybir.dt.from_np(_np.dtype(dtype))
        args.append(nc.dram_tensor(f"out_{i}_dram", shape, dt, kind="ExternalOutput").ap())
    pre_ln_arccos_attention_moe_kernel(nc, *args)
    r = _run(nc, [arrays], core_ids=[0])
    return r.results[0]["out_0_dram"]
```

```python
import concourse.bass as bass
from concourse import mybir
from contextlib import ExitStack


def pre_ln_arccos_attention_moe_kernel(nc, x, w_qkv, b_qkv, w_out, b_out, centroids, expert_biases,
                                       Wr, br, Ws, bs, out):
    fp32 = mybir.dt.float32
    bf16 = mybir.dt.bfloat16
    ALU = mybir.AluOpType
    ACT = mybir.ActivationFunctionType
    AX = mybir.AxisListType

    B, S, D = x.shape
    P = 128
    HD = 16
    H = D // HD
    NH = B * H
    KT = S // P
    BT = KT // 2
    NB = 2 * NH
    KC = D // P
    NR = Wr.shape[0]
    NS = Ws.shape[0]
    G = 4
    NG = B * S // (G * P)
    GPB = NG // B
    GT = G * P
    PI = 3.141592653589793
    CLIP = 1.0 - 1e-7
    POWER = -2.0 - 1.2
    LN_EPS = 1e-5
    TINY = 1e-12

    x_rows = x.rearrange("b s d -> (b s) d")
    out_rows = out.rearrange("b s d -> (b s) d")
    qk_parts = nc.dram_tensor("qk_parts", (2, 3, NH, HD, S), bf16, kind="Internal").ap()
    head_out = nc.dram_tensor("head_out", (NH, 4, 32, 512), fp32, kind="Internal").ap()
    row_scale = nc.dram_tensor("row_scale", (NH, 4, 512), fp32, kind="Internal").ap()

    ctx = ExitStack()
    with ctx:
        def sb(name, shape, dt):
            return ctx.enter_context(nc.sbuf_tensor(name, shape, dt))

        def pb(name, shape, dt):
            return ctx.enter_context(nc.psum_tensor(name, shape, dt))

        def sem(name):
            return ctx.enter_context(nc.semaphore(name))

        X = sb("X", [P, 2, BT, S], fp32)
        V = sb("V", [P, NH, KT, HD], fp32)
        cosc = sb("cosc", [P, 2, S], fp32)
        stacks = sb("stacks", [P, 2, 2, S], bf16)
        vp = sb("vp", [P, 4, 32], fp32)
        ncol = sb("ncol", [P, BT], fp32)
        evac = sb("evac", [P, 2, 512], fp32)
        ident = sb("ident", [P, P], fp32)
        identb = sb("identb", [P, P], bf16)
        ones = sb("ones", [1, P], fp32)
        consts = sb("consts", [P, 4], fp32)
        one_c, theta_c, eps_c = consts[:, 0:1], consts[:, 1:2], consts[:, 2:3]

        flat = X[:, :, :, :].rearrange("p a b c -> p (a b c)")
        at = [0]

        def carve(dims, dt=fp32, parts=P):
            n = 1
            for d in dims:
                n *= d
            words = n if dt == fp32 else n // 2
            v = flat[0:parts, at[0]:at[0] + words]
            at[0] += words
            assert at[0] <= 2 * BT * S
            if dt != fp32:
                v = v.bitcast(dt)
            if len(dims) == 1:
                return v
            names = "abcd"[:len(dims)]
            return v.rearrange("p (" + " ".join(names) + ") -> p " + " ".join(names),
                               **{m: d for m, d in zip(names, dims)})

        psum = pb("psum", [P, 8, 512], fp32)
        banks = [psum[:, i, :] for i in range(8)]

        w_nat = carve([6, D])
        w_t = carve([KC, 3 * D])
        bq_row = carve([3 * D], parts=1)
        xin = [carve([G, D]) for _ in range(2)]
        xn = [carve([G, D]) for _ in range(2)]
        xn_t = [carve([KC, GT]) for _ in range(2)]
        sq = [carve([2 * D]) for _ in range(2)]
        qn = [carve([2 * D]) for _ in range(2)]
        rest = [carve([2 * D]) for _ in range(2)]
        parts = [carve([3, 2 * D], bf16) for _ in range(4)]
        parts_t = [carve([12, GT], bf16) for _ in range(2)]
        stats = carve([G, 6])
        mv = carve([G, 2])
        sd = carve([G])
        rstd = carve([G])
        ssum = [carve([2 * H]) for _ in range(2)]
        norm = [carve([2 * H]) for _ in range(2)]
        rnorm = [carve([2 * H]) for _ in range(2)]
        ps_xt = banks[0:2]
        ps_qk = banks[2:4]
        ps_v = [banks[4][:, 0:D], banks[5][:, 0:D]]
        ps_pt = [banks[6][:, :].bitcast(bf16), banks[7][:, :].bitcast(bf16)]

        made = sem("made")
        w_in = sem("w_in")
        w_ps = sem("w_ps")
        w_sb = sem("w_sb")
        x_in = [sem(f"x_in{m}") for m in range(2)]
        x_used = sem("x_used")
        var_ok = sem("var_ok")
        sd_ok = sem("sd_ok")
        xn_ok = sem("xn_ok")
        xt_ps = sem("xt_ps")
        xt_ok = sem("xt_ok")
        qk_ps = sem("qk_ps")
        sq_ok = sem("sq_ok")
        ss_ok = sem("ss_ok")
        norm_ok = sem("norm_ok")
        v_ok = sem("v_ok")
        qn_ok = sem("qn_ok")
        hi_ok = sem("hi_ok")
        rest_ok = sem("rest_ok")
        mid_ok = sem("mid_ok")
        low_ok = sem("low_ok")
        pt0_ps = sem("pt0_ps")
        pt1_ps = sem("pt1_ps")
        pt0_ok = sem("pt0_ok")
        pt1_ok = sem("pt1_ok")
        parts_out = [sem(f"parts_out{m}") for m in range(2)]
        dve_step = sem("dve_step")
        un_step = sem("un_step")

        def wait(engine, semaphore, value):
            if not isinstance(value, int) or value > 0:
                engine.wait_ge(semaphore, value)

        held = sem("held")

        def hold(engine, semaphore, value):
            engine.wait_ge(semaphore, value)
            engine.sem_inc(held, 1)

        TURNS = NG // 2
        NT = NG * G

        def real(k, j):
            return not isinstance(k, int) or 0 <= 2 * G * k + j < NT

        def on(stage, k, j):
            if real(k, j):
                stage(k, j)

        def slots(engine, slot):
            for j in range(2 * G):
                slot(0, j)
            with engine.Fori(1, TURNS - 1) as k:
                for j in range(2 * G):
                    slot(k, j)
            for j in range(2 * G + 4):
                slot(TURNS - 1, j)

        with nc.Block() as block:
            @block.gpsimd
            def _(pool):
                def load(g, m):
                    pool.dma_start(xin[m], x_rows[bass.ds(g * GT, GT), :].rearrange("(j p) d -> p j d", p=P)
                                   ).then_inc(x_in[m], 16)

                load(0, 0)
                load(1, 1)
                nc.gpsimd.memset(ident[:, :], 0.0).then_inc(made, 1)
                nc.gpsimd.memset(identb[:, :], 0.0).then_inc(made, 1)
                nc.gpsimd.memset(ones[:, :], 1.0).then_inc(made, 1)
                nc.gpsimd.memset(one_c, 1.0).then_inc(made, 1)
                nc.gpsimd.memset(theta_c, 1.0 + PI / 2).then_inc(made, 1)
                nc.gpsimd.memset(eps_c, LN_EPS).then_inc(made, 1)
                nc.gpsimd.memset(vp[:, :, :], 0.0).then_inc(made, 1)
                pool.wait_ge(made, 7)
                for m in (ident, identb):
                    nc.gpsimd.affine_select(out=m[:, :], in_=m[:, :], compare_op=ALU.not_equal, fill=1.0,
                                            base=0, pattern=[[-1, P]], channel_multiplier=1).then_inc(made, 1)
                nc.gpsimd.memset(vp[:, :, 17:18], 1.0).then_inc(made, 1)
                with pool.Fori(1, TURNS) as k:
                    for m in range(2):
                        hold(pool, x_used, (2 * k + m - 1) * G)
                        load(2 * k + m, m)

            @block.sync
            def _(sp):
                sp.dma_start(w_nat, w_qkv.rearrange("(c p) d -> p c d", p=P)).then_inc(w_in, 16)
                sp.dma_start(bq_row, b_qkv.rearrange("(a n) -> a n", a=1)).then_inc(w_in, 16)

                def step(k, m):
                    hold(sp, pt0_ok, (2 * k + m) * G + G)
                    hold(sp, pt1_ok, (2 * k + m) * G + G)
                    for c in range(4):
                        for p in range(3):
                            dst = qk_parts[c // 2, p, bass.ds((k // (GPB // 2)) * H + c % 2 * 8, 8), :,
                                           bass.ds((k % (GPB // 2)) * 2 * GT + m * GT, GT)]
                            sp.dma_start(dst, parts_t[m][:, p * 4 + c, :]).then_inc(parts_out[m], 16)

                for m in range(2):
                    step(0, m)
                with sp.Fori(1, TURNS) as k:
                    for m in range(2):
                        step(k, m)
                for m in range(2):
                    sp.wait_ge(parts_out[m], TURNS * 192)

            @block.scalar
            def _(act):
                for c in range(6):
                    act.wait_ge(w_ps, c + 1)
                    nc.scalar.activation(w_t[:, :, c * P:(c + 1) * P],
                                         banks[c % 2][:, 0:KC * P].rearrange("p (k n) -> p k n", k=KC),
                                         ACT.Copy).then_inc(w_sb, 1)

                def deviations(k, m):
                    act.wait_ge(var_ok, (2 * k + m) * G + G)
                    nc.scalar.activation(sd, mv[:, :, 1], ACT.Sqrt, bias=eps_c).then_inc(sd_ok, 1)

                def copies(k, m):
                    g = 2 * k + m
                    for c in range(KC):
                        act.wait_ge(xt_ps, g * KC + c + 1)
                        if c == 0:
                            wait(act, qk_ps, (g - 1) * G)
                        nc.scalar.activation(xn_t[m % 2][:, c, :], ps_xt[c][:, :], ACT.Copy).then_inc(xt_ok, 1)

                def squares(k, j):
                    t = 2 * G * k + j
                    act.wait_ge(qk_ps, t + 1)
                    wait(act, ss_ok, t - 1)
                    nc.scalar.activation(sq[j % 2], ps_qk[j % 2], ACT.Square).then_inc(sq_ok, 1)
                    nc.scalar.activation(V[:, bass.ds((k // (GPB // 2)) * H, H),
                                           bass.ds((k % (GPB // 2)) * 2 * G + j, 1), :],
                                         ps_v[j % 2].rearrange("p (h o d) -> p h o d", h=H, o=1),
                                         ACT.Copy).then_inc(v_ok, 1)

                def norms(k, j):
                    act.wait_ge(ss_ok, 2 * G * k + j + 1)
                    nc.scalar.activation(norm[j % 2], ssum[j % 2], ACT.Sqrt).then_inc(norm_ok, 1)

                def high(k, j):
                    t = 2 * G * k + j
                    act.wait_ge(qn_ok, t + 1)
                    wait(act, pt1_ps, t - 3)
                    nc.scalar.activation(parts[j % 4][:, 0, :], qn[j % 2], ACT.Copy).then_inc(hi_ok, 1)

                def middle(k, j):
                    act.wait_ge(rest_ok, 2 * G * k + j + 1)
                    nc.scalar.activation(parts[j % 4][:, 1, :], rest[j % 2], ACT.Copy).then_inc(mid_ok, 1)

                def evacuate(k, j):
                    t = 2 * G * k + j
                    act.wait_ge(pt0_ps, t + 1)
                    if j % G == 0:
                        wait(act, parts_out[j // G % 2], (k + j // (2 * G)) * 192)
                    q = j % G * P
                    nc.scalar.activation(parts_t[j // G % 2][:, 0:8, q:q + P],
                                         ps_pt[0].rearrange("p (c n) -> p c n", c=8), ACT.Copy).then_inc(pt0_ok, 1)

                def slot(k, j):
                    on(squares, k, j)
                    if j % G == 0 and real(k, j + G):
                        deviations(k, j // G + 1)
                    on(norms, k, j - 1)
                    on(high, k, j - 2)
                    on(middle, k, j - 3)
                    on(evacuate, k, j - 4)
                    if j % G == 2 and real(k, j + G - 2):
                        copies(k, j // G + 1)

                deviations(0, 0)
                copies(0, 0)
                slots(act, slot)

            @block.vector
            def _(dve):
                def statistics(k, m):
                    g = 2 * k + m
                    dve.wait_ge(x_in[m % 2], (k + m // 2) * 16 + 16)
                    for j in range(G):
                        nc.vector.bn_stats(stats[:, j, :], xin[m % 2][:, j, :]).then_inc(dve_step, 1)
                    hold(dve, dve_step, g * (G + 1) + G)
                    for j in range(G):
                        nc.vector.bn_aggr(mv[:, j, :], stats[:, j, :]).then_inc(var_ok, 1)

                def centre(k, m):
                    g = 2 * k + m
                    dve.wait_ge(sd_ok, g + 1)
                    nc.vector.reciprocal(rstd, sd).then_inc(dve_step, 1)
                    dve.wait_ge(dve_step, g * (G + 1) + G + 1)
                    wait(dve, xt_ps, (g - 1) * KC)
                    for j in range(G):
                        nc.vector.tensor_scalar(xn[m % 2][:, j, :], xin[m % 2][:, j, :], mv[:, j, 0:1],
                                                rstd[:, j:j + 1], ALU.subtract, ALU.mult).then_inc(x_used, 1)

                def sums(k, j):
                    t = 2 * G * k + j
                    dve.wait_ge(sq_ok, t + 1)
                    wait(dve, norm_ok, t - 1)
                    nc.vector.reduce_sum(ssum[j % 2], sq[j % 2].rearrange("p (h d) -> p h d", d=HD),
                                         AX.X).then_inc(ss_ok, 1)

                def unit(k, j):
                    t = 2 * G * k + j
                    dve.wait_ge(norm_ok, t + 1)
                    nc.vector.tensor_scalar_max(norm[j % 2], norm[j % 2], TINY).then_inc(un_step, 1)
                    dve.wait_ge(un_step, t * 2 + 1)
                    nc.vector.reciprocal(rnorm[j % 2], norm[j % 2]).then_inc(un_step, 1)
                    dve.wait_ge(un_step, t * 2 + 2)
                    wait(dve, hi_ok, t - 1)
                    nc.vector.tensor_tensor(qn[j % 2].rearrange("p (h d) -> p h d", d=HD),
                                            ps_qk[j % 2].rearrange("p (h d) -> p h d", d=HD),
                                            rnorm[j % 2].unsqueeze(2).broadcast_to([P, 2 * H, HD]),
                                            ALU.mult).then_inc(qn_ok, 1)

                def remainder(k, j):
                    t = 2 * G * k + j
                    dve.wait_ge(hi_ok, t + 1)
                    wait(dve, low_ok, t - 1)
                    nc.vector.tensor_tensor(rest[j % 2], qn[j % 2], parts[j % 4][:, 0, :],
                                            ALU.subtract).then_inc(rest_ok, 1)

                def low(k, j):
                    dve.wait_ge(mid_ok, 2 * G * k + j + 1)
                    nc.vector.tensor_tensor(parts[j % 4][:, 2, :], rest[j % 2], parts[j % 4][:, 1, :],
                                            ALU.subtract).then_inc(low_ok, 1)

                def evacuate(k, j):
                    dve.wait_ge(pt1_ps, 2 * G * k + j + 1)
                    if j % G == 0:
                        wait(dve, parts_out[j // G % 2], (k + j // (2 * G)) * 192)
                    q = j % G * P
                    nc.vector.tensor_copy(parts_t[j // G % 2][:, 8:12, q:q + P],
                                          ps_pt[1][:, 0:4 * P].rearrange("p (c n) -> p c n", c=4)
                                          ).then_inc(pt1_ok, 1)

                def slot(k, j):
                    on(sums, k, j)
                    if j % G == 0 and real(k, j + G):
                        statistics(k, j // G + 1)
                    on(unit, k, j - 1)
                    on(remainder, k, j - 2)
                    on(low, k, j - 3)
                    if j % G == 1 and real(k, j + G - 1):
                        centre(k, j // G + 1)
                    on(evacuate, k, j - 4)

                statistics(0, 0)
                centre(0, 0)
                slots(dve, slot)

            @block.tensor
            def _(pe):
                pe.wait_ge(made, 10)
                pe.wait_ge(w_in, 32)
                for c in range(6):
                    if c >= 2:
                        pe.wait_ge(w_sb, c - 1)
                    for kc in range(KC):
                        last = nc.tensor.transpose(banks[c % 2][:, kc * P:(kc + 1) * P],
                                                   w_nat[:, c, kc * P:(kc + 1) * P], ident[:, :])
                    last.then_inc(w_ps, 1)
                pe.wait_ge(w_sb, 6)

                def rows_t(k, m):
                    g = 2 * k + m
                    pe.wait_ge(x_used, g * G + G)
                    wait(pe, xt_ok, g * KC)
                    for c in range(KC):
                        for j in range(G):
                            last = nc.tensor.transpose(ps_xt[c][:, j * P:(j + 1) * P],
                                                       xn[m % 2][:, j, c * P:(c + 1) * P], ident[:, :])
                        last.then_inc(xt_ps, 1)

                def project(k, j):
                    t = 2 * G * k + j
                    if j % G == 0:
                        pe.wait_ge(xt_ok, (2 * k + j // G) * KC + KC)
                    wait(pe, qn_ok, t - 1)
                    wait(pe, v_ok, t - 1)
                    q = j % G * P
                    for dst, a, b in ((ps_qk[j % 2], 0, 2 * D), (ps_v[j % 2], 2 * D, 3 * D)):
                        for c in range(KC):
                            nc.tensor.matmul(dst, xn_t[j // G][:, c, q:q + P], w_t[:, c, a:b],
                                             start=(c == 0), stop=False)
                        mm = nc.tensor.matmul(dst, ones[0:1, :], bq_row[0:1, a:b], start=False, stop=True)
                    mm.then_inc(qk_ps, 1)

                def parts_rows(k, j):
                    t = 2 * G * k + j
                    pe.wait_ge(low_ok, t + 1)
                    for half, (ok, ps) in enumerate(((pt0_ok, pt0_ps), (pt1_ok, pt1_ps))):
                        wait(pe, ok, t)
                        for b in range(8 * half, 8 + 4 * half):
                            mm = nc.tensor.transpose(ps_pt[half][:, (b - 8 * half) * P:(b - 8 * half + 1) * P],
                                                     parts[j % 4][:, b // 4, b % 4 * P:(b % 4 + 1) * P],
                                                     identb[:, :])
                        mm.then_inc(ps, 1)

                def slot(k, j):
                    on(project, k, j)
                    if j % G == 2 and real(k, j + G - 2):
                        rows_t(k, j // G + 1)
                    on(parts_rows, k, j - 4)

                rows_t(0, 0)
                slots(pe, slot)

        nc.disable_value_cache = True
        ps_sum = banks[0]
        ps_clip = banks[1:3]
        ps_mult = banks[3:5]

        stack_in = sem("stack_in")
        clip_ps = sem("clip_ps")
        clip_ok = sem("clip_ok")
        square_ok = sem("square_ok")
        log_ok = sem("log_ok")
        recip_ok = sem("recip_ok")
        mult_ps = sem("mult_ps")
        mult_ok = sem("mult_ok")
        atan_ok = sem("atan_ok")
        log2_ok = sem("log2_ok")
        score_ok = sem("score_ok")
        nc_ok = sem("nc_ok")
        vp_ok = sem("vp_ok")
        sum_ps = sem("sum_ps")
        sum_ok = sem("sum_ok")
        head_stored = [sem(f"head_stored{h}") for h in range(2)]
        LOADS = 11 * 16
        LAST = NB // 4 - 1
        BEFORE, AFTER = (4, 5), (6, 7)
        RECIP_STARTS = (0, 1, 2, 4, 6)

        def periods(engine, emit):
            for m in range(4):
                emit(0, m)
            with engine.Fori(1, LAST) as k:
                for m in range(4):
                    emit(k, m)
            for m in range(4):
                emit(LAST, m)

        def has(k, m):
            return not (isinstance(k, int) and 4 * k + m >= NB)

        with nc.Block() as block:
            @block.sync
            def _(sp):
                def load(k, h):
                    head, buf = 2 * k + h, h % 2
                    row = 0
                    for part, times in ((0, 3), (1, 3), (2, 2)):
                        for _ in range(times):
                            sp.dma_start(stacks[row:row + HD, 0, buf, :],
                                         qk_parts[0, part, bass.ds(head, 1), :, :].rearrange("o d s -> (o d) s")
                                         ).then_inc(stack_in, 16)
                            row += HD
                    for row, n in ((0, 3), (3, 3), (6, 2)):
                        sp.dma_start(stacks[row * HD:(row + n) * HD, 1, buf, :],
                                     qk_parts[1, 0:n, bass.ds(head, 1), :, :].rearrange("p o d s -> (p o) d s")
                                     ).then_inc(stack_in, 16)

                def emit(k, m):
                    n = 4 * k + m
                    if m % 2 == 0:
                        if has(k, m + 4):
                            hold(sp, mult_ok, (n + 2) * 4 * BT)
                            load(k, m // 2 + 2)
                    else:
                        head = 2 * k + m // 2
                        hold(sp, sum_ok, head + 1)
                        sp.dma_start(head_out[bass.ds(head, 1)].rearrange("o j r s -> (o j r) s"),
                                     evac[:, m // 2, :]).then_inc(head_stored[m // 2], 16)

                load(0, 0)
                load(0, 1)
                periods(sp, emit)
                for h in range(2):
                    sp.wait_ge(head_stored[h], NH // 2 * 16)

            @block.tensor
            def _(pe):
                def cosines(dst, m, i, q0, n):
                    buf = m // 2 % 2
                    keys = (m % 2 * BT + i) * P
                    return nc.tensor.matmul(dst, stacks[:, 1, buf, keys:keys + P],
                                            stacks[:, 0, buf, q0:q0 + n], start=True, stop=True)

                def clip(k, m, i):
                    for j in range(4):
                        wait(pe, clip_ok, ((4 * k + m) * BT + i) * 4 + j - 1)
                        cosines(ps_clip[j % 2], m, i, j * 512, 512).then_inc(clip_ps, 1)

                def mult(k, m, i):
                    for j in range(4):
                        wait(pe, mult_ok, ((4 * k + m) * BT + i) * 4 + j - 1)
                        cosines(ps_mult[j % 2], m, i, j * 512, 512).then_inc(mult_ps, 1)

                def add(k, m, i):
                    t = (4 * k + m) * BT + i
                    pe.wait_ge(vp_ok, t + 1)
                    if m % 2 == 0 and i == 0:
                        wait(pe, sum_ok, 2 * k + m // 2)
                    for j in range(4):
                        mm = nc.tensor.matmul(ps_sum[32 * j:32 * j + 32, :], vp[:, i % 4, :],
                                              X[:, m % 2, i, j * 512:(j + 1) * 512],
                                              start=(m % 2 == 0 and i == 0), stop=(m % 2 == 1 and i == BT - 1),
                                              tile_position=(0, 32 * j))
                    mm.then_inc(sum_ps, 1)

                def emit(k, m):
                    if m % 2 == 0 and has(k, m + 2):
                        pe.wait_ge(stack_in, (2 * k + m // 2 + 2) * LOADS)
                    for i in range(BT // 2):
                        if has(k, m + 2):
                            clip(k, m + 2, i)
                        add(k, m, 2 * i)
                        add(k, m, 2 * i + 1)
                    if has(k, m + 2):
                        for i in BEFORE:
                            clip(k, m + 2, i)
                    if has(k, m + 1):
                        for i in range(BT):
                            mult(k, m + 1, i)
                    if has(k, m + 2):
                        for i in AFTER:
                            clip(k, m + 2, i)

                pe.wait_ge(stack_in, 2 * LOADS)
                for i in range(BT):
                    clip(0, 0, i)
                for i in range(BT):
                    clip(0, 1, i)
                    mult(0, 0, i)
                periods(pe, emit)

            @block.vector
            def _(dve):
                def clip(k, m, i):
                    t = (4 * k + m) * BT + i
                    wait(dve, square_ok, t - 1)
                    for j in range(4):
                        dve.wait_ge(clip_ps, t * 4 + j + 1)
                        nc.vector.tensor_scalar(cosc[:, i % 2, j * 512:(j + 1) * 512], ps_clip[j % 2],
                                                -CLIP, CLIP, ALU.max, ALU.min).then_inc(clip_ok, 1)

                def mult(k, m, i):
                    t = (4 * k + m) * BT + i
                    if i in RECIP_STARTS:
                        dve.wait_ge(recip_ok, (4 * k + m) * len(RECIP_STARTS) + RECIP_STARTS.index(i) + 1)
                    for j in range(4):
                        dve.wait_ge(mult_ps, t * 4 + j + 1)
                        part = X[:, m % 2, i, j * 512:(j + 1) * 512]
                        nc.vector.tensor_tensor(part, ps_mult[j % 2], part, ALU.mult).then_inc(mult_ok, 1)

                def values(k, m, i):
                    t = (4 * k + m) * BT + i
                    dve.wait_ge(score_ok, t + 1)
                    wait(dve, sum_ps, t - 3)
                    nc.vector.reciprocal(vp[:, i % 4, HD:HD + 1], ncol[:, i:i + 1]).then_inc(nc_ok, 1)
                    dve.wait_ge(nc_ok, t + 1)
                    nc.vector.tensor_scalar(vp[:, i % 4, 0:HD],
                                            V[:, bass.ds(2 * k + m // 2, 1), m % 2 * BT + i, :].rearrange(
                                                "p o d -> p (o d)"),
                                            vp[:, i % 4, HD:HD + 1], None, ALU.mult).then_inc(vp_ok, 1)

                def emit(k, m):
                    for i in range(BT // 2):
                        values(k, m, 2 * i)
                        values(k, m, 2 * i + 1)
                        if has(k, m + 2):
                            clip(k, m + 2, i)
                    if has(k, m + 2):
                        for i in BEFORE:
                            clip(k, m + 2, i)
                    if has(k, m + 1):
                        for i in range(BT):
                            mult(k, m + 1, i)
                    if has(k, m + 2):
                        for i in AFTER:
                            clip(k, m + 2, i)
                    if m % 2 == 1:
                        head = 2 * k + m // 2
                        dve.wait_ge(sum_ps, (head + 1) * KT)
                        wait(dve, head_stored[m // 2], k * 16)
                        nc.vector.tensor_copy(evac[:, m // 2, :], ps_sum).then_inc(sum_ok, 1)

                for i in range(BT):
                    clip(0, 0, i)
                for i in range(BT):
                    clip(0, 1, i)
                    mult(0, 0, i)
                periods(dve, emit)

            @block.gpsimd
            def _(pool):
                def square(k, m, i):
                    t = (4 * k + m) * BT + i
                    pool.wait_ge(clip_ok, t * 4 + 4)
                    wait(pool, sum_ps, t - 2 * BT + 1)
                    nc.gpsimd.tensor_tensor(X[:, m % 2, i, :], cosc[:, i % 2, :], cosc[:, i % 2, :],
                                            ALU.mult).then_inc(square_ok, 1)

                def emit(k, m):
                    if has(k, m + 2):
                        for i in range(BT):
                            square(k, m + 2, i)

                for m in range(2):
                    for i in range(BT):
                        square(0, m, i)
                periods(pool, emit)

            @block.scalar
            def _(act):
                def tiles(m, a, b):
                    return X[:, m % 2, a:b, :]

                def sines(k, m):
                    n = 4 * k + m
                    for i in range(2):
                        act.wait_ge(square_ok, n * BT + (i + 1) * 4)
                        own = tiles(m, 4 * i, 4 * i + 4)
                        nc.scalar.activation(own, own, ACT.Ln, bias=one_c, scale=-1.0).then_inc(log_ok, 1)
                    for a, b in zip(RECIP_STARTS, RECIP_STARTS[1:] + (BT,)):
                        act.wait_ge(log_ok, n * 2 + a // 4 + 1)
                        own = tiles(m, a, b)
                        nc.scalar.activation(own, own, ACT.Sigmoid, scale=-0.5).then_inc(recip_ok, 1)
                    for i in range(4):
                        act.wait_ge(mult_ok, (n * BT + 2 * i + 2) * 4)
                        own = tiles(m, 2 * i, 2 * i + 2)
                        nc.scalar.activation(own, own, ACT.Arctan).then_inc(atan_ok, 1)

                def scores(k, m):
                    n = 4 * k + m
                    nc.scalar.preload_act_table_set("natural_log_exp_and_others")
                    for i in range(2):
                        act.wait_ge(atan_ok, n * 4 + 2 * i + 2)
                        own = tiles(m, 4 * i, 4 * i + 4)
                        nc.scalar.activation(own, own, ACT.Ln, bias=theta_c, scale=-2.0).then_inc(log2_ok, 1)
                    for i in range(BT):
                        act.wait_ge(log2_ok, n * 2 + i // 4 + 1)
                        nc.scalar.activation(X[:, m % 2, i, :], X[:, m % 2, i, :], ACT.Exp, scale=POWER,
                                             accum_out=ncol[:, i:i + 1]).then_inc(score_ok, 1)

                def emit(k, m):
                    scores(k, m)
                    if has(k, m + 1):
                        sines(k, m + 1)

                sines(0, 0)
                periods(act, emit)

        at[0] = 0
        NE = NR + 1
        NW = NE * D
        NX = NR + NS
        wr_nat = carve([NR, KC, D])
        ws_nat = carve([NS, KC, D])
        ws_sum = carve([KC, D])
        we_t = carve([KC, NW])
        wo_nat = carve([KC, D])
        wo_t = carve([KC, D])
        cen_nat = carve([D], parts=NR)
        cen_t = carve([KC, NR])
        bo_row = carve([D], parts=1)
        eb_row = carve([NR], parts=1)
        be_rows = carve([D], parts=NX)
        order = carve([NR])
        den = carve([512])
        nrow = carve([512])
        scl = carve([512])
        raw = carve([KC, GT])
        scale_b = carve([KC, GT])
        attn = carve([KC, GT])
        xres = carve([G, D])
        x1 = carve([D])
        u = carve([D])
        acc = [carve([D]) for _ in range(2)]
        u_t = [carve([KC, P]) for _ in range(2)]
        gate = [carve([NX]) for _ in range(2)]
        gate_t = [carve([P], parts=NX) for _ in range(2)]
        stat = carve([6])
        mean = carve([2])
        dev = carve([1])
        rdev = carve([1])
        top = carve([1])
        neg_top = carve([1])
        expd = carve([NR])
        esum = carve([1])
        resum = carve([1])
        prob = carve([NR])
        m1 = carve([1])
        t1 = carve([NR])
        w1 = carve([1])
        f1 = carve([NR])
        p2 = carve([NR])
        m2 = carve([1])
        t2 = carve([NR])
        w2 = carve([1])
        f2 = carve([NR])
        ps_e = banks[0:3]
        ps_y, ps_u, ps_l, ps_g = banks[3], banks[4], banks[5], banks[6]
        ps_l = ps_l[:, 0:NR]

        t_in = sem("t_in")
        t_sums = sem("t_sums")
        t_made = sem("t_made")
        t_ws = sem("t_ws")
        t_ps = sem("t_ps")
        t_sb = sem("t_sb")
        scale_ok = sem("scale_ok")
        scale_out = sem("scale_out")
        raw_in = sem("raw_in")
        xres_in = sem("xres_in")
        attn_ok = sem("attn_ok")
        y_ps = sem("y_ps")
        x1_ok = sem("x1_ok")
        var2_ok = sem("var2_ok")
        dev_ok = sem("dev_ok")
        u_ok = sem("u_ok")
        acc0_ok = sem("acc0_ok")
        u_ps = sem("u_ps")
        ut_ok = sem("ut_ok")
        l_ps = sem("l_ps")
        top_ok = sem("top_ok")
        exp_ok = sem("exp_ok")
        gate_ok = sem("gate_ok")
        g_ps = sem("g_ps")
        gt_ok = sem("gt_ok")
        e_ps = sem("e_ps")
        e_ok = sem("e_ok")
        rows_out = sem("rows_out")
        chain3 = sem("chain3")

        def blocks(engine, emit):
            emit(0)
            with engine.Fori(1, NG - 1) as k:
                emit(k)
            emit(NG - 1)

        def final(k, j):
            return isinstance(k, int) and k == NG - 1 and j == G - 1

        with nc.Block() as block:
            @block.gpsimd
            def _(pool):
                for e in range(NR):
                    nc.gpsimd.memset(order[:, e:e + 1], float(NR - e)).then_inc(t_made, 1)
                for g in gate:
                    nc.gpsimd.memset(g[:, NR:NX], 1.0 / NS).then_inc(t_made, 1)

            @block.sync
            def _(sp):
                sp.dma_start(den, head_out[:, :, HD, :].rearrange("h j s -> (h j) s")).then_inc(t_sums, 16)
                sp.dma_start(nrow, head_out[:, :, HD + 1, :].rearrange("h j s -> (h j) s")).then_inc(t_sums, 16)
                sp.dma_start(ws_nat.rearrange("p e c d -> p (e c) d"),
                             Ws.rearrange("e (c p) d -> p (e c) d", p=P)).then_inc(t_ws, 16)
                sp.dma_start(wo_nat, w_out.rearrange("(c p) d -> p c d", p=P)).then_inc(t_in, 16)
                sp.dma_start(cen_nat, centroids).then_inc(t_in, 16)
                sp.dma_start(bo_row, b_out.rearrange("(a n) -> a n", a=1)).then_inc(t_in, 16)
                sp.dma_start(eb_row, expert_biases.rearrange("(a n) -> a n", a=1)).then_inc(t_in, 16)
                sp.dma_start(be_rows[0:NR, :], br).then_inc(t_in, 16)
                sp.dma_start(be_rows[NR:NX, :], bs).then_inc(t_in, 16)
                sp.dma_start(wr_nat.rearrange("p e c d -> p (e c) d"),
                             Wr.rearrange("e (c p) d -> p (e c) d", p=P)).then_inc(t_in, 16)
                sp.wait_ge(scale_ok, 1)
                sp.dma_start(row_scale.rearrange("h j s -> (h j) s"), scl).then_inc(scale_out, 16)
                sp.wait_ge(scale_out, 16)

                def load_raw(k):
                    for c in range(KC):
                        heads = bass.ds((k // GPB) * H + c * 8, 8)
                        sp.dma_start(raw[:, c, :], head_out[heads, bass.ds(k % GPB, 1), 0:HD, :].rearrange(
                            "h o r s -> (h o) r s")).then_inc(raw_in, 16)
                        sp.dma_start(scale_b[:, c, :], row_scale[heads, bass.ds(k % GPB, 1), :].broadcast_to(
                            [8, HD, 512])).then_inc(raw_in, 16)

                def load_x(k):
                    sp.dma_start(xres, x_rows[bass.ds(k * GT, GT), :].rearrange("(j p) d -> p j d", p=P)
                                 ).then_inc(xres_in, 16)

                def store(k, j):
                    hold(sp, e_ok, (k * G + j + 1) * NE)
                    sp.dma_start(out_rows[bass.ds((k * G + j) * P, P), :], acc[j % 2]).then_inc(rows_out, 16)
                    hold(sp, rows_out, (k * G + j + 1) * 16)

                def emit(k):
                    last = isinstance(k, int) and k == NG - 1
                    if not last:
                        hold(sp, attn_ok, k * KC + KC)
                        load_raw(k + 1)
                    for j in range(G):
                        store(k, j)
                        if j == G - 2 and not last:
                            hold(sp, x1_ok, (k + 1) * G)
                            load_x(k + 1)

                load_raw(0)
                load_x(0)
                blocks(sp, emit)

            @block.tensor
            def _(pe):
                n = 0
                pe.wait_ge(t_in, 7 * 16)
                pe.wait_ge(t_made, NR + 2)
                pe.wait_ge(chain3, 1)
                for e in range(NE):
                    if e >= 2:
                        pe.wait_ge(t_sb, e - 1)
                    for dc in range(KC):
                        for oc in range(KC):
                            nat = wr_nat[:, e, oc, dc * P:(dc + 1) * P] if e < NR else ws_sum[:, oc, dc * P:(dc + 1) * P]
                            mm = nc.tensor.transpose(ps_e[e % 2][:, (dc * KC + oc) * P:(dc * KC + oc + 1) * P],
                                                     nat, ident[:, :])
                    mm.then_inc(t_ps, 1)
                for dc in range(KC):
                    for oc in range(KC):
                        mm = nc.tensor.transpose(ps_y[:, (dc * KC + oc) * P:(dc * KC + oc + 1) * P],
                                                 wo_nat[:, oc, dc * P:(dc + 1) * P], ident[:, :])
                mm.then_inc(t_ps, 1)
                for dc in range(KC):
                    mm = nc.tensor.transpose(ps_u[:, dc * NR:(dc + 1) * NR], cen_nat[:, dc * P:(dc + 1) * P],
                                             ident[0:NR, 0:NR])
                mm.then_inc(t_ps, 1)
                pe.wait_ge(t_sb, NE + 2)

                def y(k, j):
                    t = k * G + j
                    if j == 0:
                        pe.wait_ge(attn_ok, k * KC + KC)
                    wait(pe, x1_ok, t)
                    for c in range(KC):
                        nc.tensor.matmul(ps_y[:, 0:D], attn[:, c, j * P:(j + 1) * P], wo_t[:, c, :],
                                         start=(c == 0), stop=False)
                    nc.tensor.matmul(ps_y[:, 0:D], ones[0:1, :], bo_row[0:1, :], start=False,
                                     stop=True).then_inc(y_ps, 1)

                def u_rows(k, j):
                    t = k * G + j
                    pe.wait_ge(u_ok, t + 1)
                    wait(pe, ut_ok, t)
                    for c in range(KC):
                        mm = nc.tensor.transpose(ps_u[:, c * P:(c + 1) * P], u[:, c * P:(c + 1) * P], ident[:, :])
                    mm.then_inc(u_ps, 1)

                def logits(k, j):
                    t = k * G + j
                    pe.wait_ge(ut_ok, t + 1)
                    wait(pe, exp_ok, t)
                    for c in range(KC):
                        nc.tensor.matmul(ps_l, u_t[j % 2][:, c, :], cen_t[:, c, :], start=(c == 0), stop=False)
                    nc.tensor.matmul(ps_l, ones[0:1, :], eb_row[0:1, :], start=False, stop=True).then_inc(l_ps, 1)

                def gates(k, j):
                    t = k * G + j
                    pe.wait_ge(gate_ok, t + 1)
                    wait(pe, gt_ok, t)
                    nc.tensor.transpose(ps_g[0:NX, 0:P], gate[j % 2], ident[:, :]).then_inc(g_ps, 1)

                def experts(k, j, c):
                    wait(pe, e_ok, (k * G + j) * NE + (-3, -1, 0, 2, 4, 6, 8, 10, 12)[c])
                    wide = 2 * D if c < NR // 2 else D
                    dst = ps_e[c % 3][:, 0:wide]
                    for kc in range(KC):
                        mm = nc.tensor.matmul(dst, u_t[j % 2][:, kc, :], we_t[:, kc, c * 2 * D:c * 2 * D + wide],
                                              start=(kc == 0), stop=(kc == KC - 1 and wide == 2 * D))
                    if wide == D:
                        pe.wait_ge(gt_ok, k * G + j + 1)
                        mm = nc.tensor.matmul(dst, gate_t[j % 2], be_rows, start=False, stop=True)
                    mm.then_inc(e_ps, 1)

                y(0, 0)
                u_rows(0, 0)
                logits(0, 0)
                gates(0, 0)

                def emit(k):
                    for j in range(G):
                        nk, nj = (k, j + 1) if j < G - 1 else (k + 1, 0)
                        more = not final(k, j)
                        if more:
                            y(nk, nj)
                        for c in range(3):
                            experts(k, j, c)
                        if more:
                            u_rows(nk, nj)
                        for c in range(3, 5):
                            experts(k, j, c)
                        if more:
                            logits(nk, nj)
                        for c in range(5, 9):
                            experts(k, j, c)
                        if more:
                            gates(nk, nj)

                blocks(pe, emit)

            @block.scalar
            def _(act):
                for e in range(0, NE, 2):
                    act.wait_ge(t_ps, e + 1)
                    if e:
                        act.wait_ge(t_sb, e)
                    nc.scalar.activation(we_t[:, :, e * D:(e + 1) * D],
                                         ps_e[e % 2][:, :].rearrange("p (k n) -> p k n", k=KC), ACT.Copy,
                                         scale=1.0 if e < NR else 1.0 / NS).then_inc(t_sb, 1)

                def sd3(k, j):
                    act.wait_ge(var2_ok, k * G + j + 1)
                    nc.scalar.activation(dev, mean[:, 1:2], ACT.Sqrt, bias=eps_c).then_inc(dev_ok, 1)

                def ut(k, j):
                    t = k * G + j
                    act.wait_ge(u_ps, t + 1)
                    wait(act, e_ps, (t - 1) * 9)
                    nc.scalar.activation(u_t[j % 2], ps_u[:, 0:D].rearrange("p (k n) -> p k n", k=KC),
                                         ACT.Copy).then_inc(ut_ok, 1)

                def exps(k, j):
                    act.wait_ge(top_ok, k * G + j + 1)
                    nc.scalar.activation(expd, ps_l, ACT.Exp, bias=neg_top, accum_out=esum).then_inc(exp_ok, 1)

                def gt(k, j):
                    act.wait_ge(g_ps, k * G + j + 1)
                    nc.scalar.activation(gate_t[j % 2], ps_g[0:NX, 0:P], ACT.Copy).then_inc(gt_ok, 1)

                def tile(k, j):
                    sd3(k, j)
                    ut(k, j)
                    exps(k, j)
                    gt(k, j)

                def emit(k):
                    for j in range(G):
                        if not final(k, j):
                            tile(*((k, j + 1) if j < G - 1 else (k + 1, 0)))

                tile(0, 0)
                blocks(act, emit)

            @block.vector
            def _(dve):
                count = [0]

                def link(ins):
                    count[0] = count[0] + 1
                    ins.then_inc(chain3, 1)
                    dve.wait_ge(chain3, count[0])

                dve.wait_ge(t_ws, 16)
                link(nc.vector.tensor_tensor(ws_sum, ws_nat[:, 0, :, :], ws_nat[:, 1, :, :], ALU.add))
                dve.wait_ge(t_sums, 32)
                link(nc.vector.reciprocal(nrow, nrow))
                link(nc.vector.tensor_tensor(den, den, nrow, ALU.mult))
                link(nc.vector.tensor_scalar_max(den, den, TINY))
                link(nc.vector.reciprocal(den, den))
                nc.vector.tensor_tensor(scl, den, nrow, ALU.mult).then_inc(scale_ok, 1)
                for e in range(1, NE, 2):
                    dve.wait_ge(t_ps, e + 1)
                    dve.wait_ge(t_sb, e)
                    nc.vector.tensor_copy(we_t[:, :, e * D:(e + 1) * D],
                                          ps_e[e % 2][:, :].rearrange("p (k n) -> p k n", k=KC)).then_inc(t_sb, 1)
                dve.wait_ge(t_ps, NE + 2)
                nc.vector.tensor_copy(wo_t, ps_y[:, :].rearrange("p (k n) -> p k n", k=KC)).then_inc(t_sb, 1)
                nc.vector.tensor_copy(cen_t, ps_u[:, 0:KC * NR].rearrange("p (k n) -> p k n", k=KC)
                                      ).then_inc(t_sb, 1)

                def scaled(k):
                    dve.wait_ge(raw_in, (k + 1) * 4 * 16)
                    wait(dve, y_ps, k * G)
                    for c in range(KC):
                        nc.vector.tensor_tensor(attn[:, c, :], raw[:, c, :], scale_b[:, c, :],
                                                ALU.mult).then_inc(attn_ok, 1)

                def residual(k, j):
                    t = k * G + j
                    if j == 0:
                        dve.wait_ge(xres_in, (k + 1) * 16)
                    dve.wait_ge(y_ps, t + 1)
                    nc.vector.tensor_tensor(x1, ps_y[:, 0:D], xres[:, j, :], ALU.add).then_inc(x1_ok, 1)
                    dve.wait_ge(x1_ok, t + 1)
                    link(nc.vector.bn_stats(stat, x1))
                    dve.sem_inc(held, 1)
                    nc.vector.bn_aggr(mean, stat).then_inc(var2_ok, 1)

                def centred(k, j):
                    t = k * G + j
                    dve.wait_ge(dev_ok, t + 1)
                    link(nc.vector.reciprocal(rdev, dev))
                    wait(dve, u_ps, t)
                    nc.vector.tensor_scalar(u, x1, mean[:, 0:1], rdev, ALU.subtract, ALU.mult).then_inc(u_ok, 1)
                    dve.wait_ge(u_ok, t + 1)
                    wait(dve, rows_out, (t - 1) * 16)
                    link(nc.vector.tensor_tensor(acc[j % 2], x1, u, ALU.add))

                def highest(k, j):
                    dve.wait_ge(l_ps, k * G + j + 1)
                    link(nc.vector.reduce_max(top, ps_l, AX.X))
                    nc.vector.tensor_scalar(neg_top, top, -1.0, None, ALU.mult).then_inc(top_ok, 1)

                def choose(k, j):
                    t = k * G + j
                    dve.wait_ge(exp_ok, t + 1)
                    link(nc.vector.reciprocal(resum, esum))
                    link(nc.vector.tensor_scalar(prob, expd, resum, None, ALU.mult))
                    link(nc.vector.reduce_max(m1, prob, AX.X))
                    link(nc.vector.scalar_tensor_tensor(t1, prob, m1, order, ALU.is_equal, ALU.mult))
                    link(nc.vector.reduce_max(w1, t1, AX.X))
                    link(nc.vector.tensor_scalar(f1, t1, w1, None, ALU.is_equal))
                    link(nc.vector.scalar_tensor_tensor(p2, f1, -2.0, prob, ALU.mult, ALU.add))
                    link(nc.vector.reduce_max(m2, p2, AX.X))
                    link(nc.vector.scalar_tensor_tensor(t2, p2, m2, order, ALU.is_equal, ALU.mult))
                    link(nc.vector.reduce_max(w2, t2, AX.X))
                    link(nc.vector.scalar_tensor_tensor(f2, t2, w2, f1, ALU.is_equal, ALU.add))
                    wait(dve, g_ps, t - 1)
                    nc.vector.tensor_tensor(gate[j % 2][:, 0:NR], prob, f2, ALU.mult).then_inc(gate_ok, 1)
                    dve.wait_ge(gate_ok, t + 1)

                def gather(k, j, c):
                    t = k * G + j
                    dve.wait_ge(e_ps, t * 9 + c + 1)
                    bank = ps_e[c % 3]
                    if c == NR // 2:
                        nc.vector.tensor_tensor(acc[j % 2], bank[:, 0:D], acc[j % 2], ALU.add).then_inc(e_ok, 1)
                        dve.wait_ge(e_ok, (t + 1) * NE)
                        return
                    for h in range(2):
                        e = 2 * c + h
                        nc.vector.scalar_tensor_tensor(acc[j % 2], bank[:, h * D:(h + 1) * D],
                                                       gate[j % 2][:, e:e + 1], acc[j % 2],
                                                       ALU.mult, ALU.add).then_inc(e_ok, 1)
                        dve.wait_ge(e_ok, t * NE + e + 1)

                scaled(0)
                residual(0, 0)
                centred(0, 0)
                highest(0, 0)
                choose(0, 0)
                start = count[0]
                per = [0]

                def emit(k):
                    if not isinstance(k, int) or k:
                        count[0] = start + k * per[0]
                    for j in range(G):
                        nk, nj = (k, j + 1) if j < G - 1 else (k + 1, 0)
                        more = not final(k, j)
                        if more:
                            if nj == 0:
                                scaled(nk)
                            residual(nk, nj)
                        gather(k, j, 0)
                        gather(k, j, 1)
                        if more:
                            centred(nk, nj)
                        gather(k, j, 2)
                        gather(k, j, 3)
                        gather(k, j, 4)
                        if more:
                            highest(nk, nj)
                        gather(k, j, 5)
                        if more:
                            choose(nk, nj)
                        for c in range(6, 9):
                            gather(k, j, c)
                    if isinstance(k, int) and k == 0:
                        per[0] = count[0] - start

                blocks(dve, emit)


_INS = ['L0_attn_x', 'L0_attn_w_qkv', 'L0_attn_b_qkv', 'L0_attn_w_out', 'L0_attn_b_out', 'L0_ffn_centroids',
        'L0_ffn_expert_biases', 'L0_ffn_Wr', 'L0_ffn_br', 'L0_ffn_Ws', 'L0_ffn_bs']
_OUTS = [((2, 2048, 256), 'float32')]


def kernel(**inputs):
    import numpy as _np
    import concourse.bacc as _bacc
    from concourse import mybir as _mybir
    from concourse.bass_utils import run_bass_kernel_spmd as _run

    nc = _bacc.Bacc("TRN2", target_bir_lowering=False, num_devices=1)
    arrays, args = {}, []
    for name in _INS:
        a = _np.ascontiguousarray(inputs[name])
        arrays[f"in_{name}_dram"] = a
        args.append(nc.dram_tensor(f"in_{name}_dram", a.shape, _mybir.dt.from_np(a.dtype), kind="ExternalInput").ap())
    for i, (shape, dtype) in enumerate(_OUTS):
        dt = _mybir.dt.from_np(_np.dtype(dtype))
        args.append(nc.dram_tensor(f"out_{i}_dram", shape, dt, kind="ExternalOutput").ap())
    pre_ln_arccos_attention_moe_kernel(nc, *args)
    r = _run(nc, [arrays], core_ids=[0])
    return r.results[0]["out_0_dram"]
```

```python
import concourse.bass as bass
from concourse import mybir
from contextlib import ExitStack


def pre_ln_arccos_attention_moe_kernel(nc, x, w_qkv, b_qkv, w_out, b_out, centroids, expert_biases,
                                       Wr, br, Ws, bs, out):
    fp32 = mybir.dt.float32
    bf16 = mybir.dt.bfloat16
    ALU = mybir.AluOpType
    ACT = mybir.ActivationFunctionType
    AX = mybir.AxisListType

    B, S, D = x.shape
    P = 128
    HD = 16
    H = D // HD
    NH = B * H
    KT = S // P
    BT = KT // 2
    NB = 2 * NH
    KC = D // P
    NR = Wr.shape[0]
    NS = Ws.shape[0]
    G = 4
    NG = B * S // (G * P)
    GPB = NG // B
    GT = G * P
    PI = 3.141592653589793
    CLIP = 1.0 - 1e-7
    POWER = -2.0 - 1.2
    LN_EPS = 1e-5
    TINY = 1e-12

    x_rows = x.rearrange("b s d -> (b s) d")
    out_rows = out.rearrange("b s d -> (b s) d")
    qk_parts = nc.dram_tensor("qk_parts", (2, 3, NH, HD, S), bf16, kind="Internal").ap()
    head_out = nc.dram_tensor("head_out", (NH, 4, 32, 512), fp32, kind="Internal").ap()
    row_scale = nc.dram_tensor("row_scale", (NH, 4, 512), fp32, kind="Internal").ap()
    NE = NR + 1
    NC = (NE + 1) // 2
    NX = NR + NS
    expert_w = nc.dram_tensor("expert_w", (NC, P, KC, 2 * D), fp32, kind="Internal").ap()

    ctx = ExitStack()
    with ctx:
        def sb(name, shape, dt):
            return ctx.enter_context(nc.sbuf_tensor(name, shape, dt))

        def pb(name, shape, dt):
            return ctx.enter_context(nc.psum_tensor(name, shape, dt))

        def sem(name):
            return ctx.enter_context(nc.semaphore(name))

        X = sb("X", [P, 2, BT, S], fp32)
        V = sb("V", [P, NH, KT, HD], fp32)
        cosc = sb("cosc", [P, 2, S], fp32)
        stacks = sb("stacks", [P, 2, 2, S], bf16)
        vp = sb("vp", [P, 4, 32], fp32)
        ncol = sb("ncol", [P, BT], fp32)
        evac = sb("evac", [P, 512], fp32)
        wo_t = sb("wo_t", [P, KC, D], fp32)
        cen_t = sb("cen_t", [P, KC, NR], fp32)
        NBIAS = 4 * D + NR
        bias3 = sb("bias3", [3, NBIAS], bf16)
        ones3 = sb("ones3", [3, P], bf16)
        be_rows = sb("be_rows", [NX, D], fp32)
        order = sb("order", [P, NR], fp32)
        rows2 = sb("rows2", [P, 2, D], fp32)
        u2_t = sb("u2_t", [P, 2, KC, P], fp32)
        gate2 = sb("gate2", [P, 2, NX], fp32)
        gate2_t = sb("gate2_t", [NX, 2, P], fp32)
        small2 = sb("small2", [P, 256], fp32)
        ident = sb("ident", [P, P], fp32)
        identb = sb("identb", [P, P], bf16)
        consts = sb("consts", [P, 4], fp32)
        one_c, theta_c, eps_c = consts[:, 0:1], consts[:, 1:2], consts[:, 2:3]

        flat = X[:, :, :, :].rearrange("p a b c -> p (a b c)")
        at = [0]

        def carve(dims, dt=fp32, parts=P):
            n = 1
            for d in dims:
                n *= d
            words = n if dt == fp32 else n // 2
            v = flat[0:parts, at[0]:at[0] + words]
            at[0] += words
            assert at[0] <= 2 * BT * S
            if dt != fp32:
                v = v.bitcast(dt)
            if len(dims) == 1:
                return v
            names = "abcd"[:len(dims)]
            return v.rearrange("p (" + " ".join(names) + ") -> p " + " ".join(names),
                               **{m: d for m, d in zip(names, dims)})

        psum = pb("psum", [P, 8, 512], fp32)
        banks = [psum[:, i, :] for i in range(8)]

        w_nat = carve([6, D])
        w_t = carve([KC, 3 * D])
        bias_row = carve([NBIAS], parts=1)
        bias_part = [carve([NBIAS], bf16, parts=1) for _ in range(3)]
        xin = [carve([G, D]) for _ in range(2)]
        xn = [carve([G, D]) for _ in range(2)]
        xn_t = [carve([KC, GT]) for _ in range(2)]
        sq = [carve([2 * D]) for _ in range(2)]
        qn = [carve([2 * D]) for _ in range(2)]
        rest = [carve([2 * D]) for _ in range(2)]
        parts = [carve([3, 2 * D], bf16) for _ in range(4)]
        parts_t = [carve([12, GT], bf16) for _ in range(2)]
        stats = carve([G, 6])
        mv = carve([G, 2])
        cen_nat = carve([D], parts=NR)
        wo_nat = carve([KC, D])
        sd = carve([G])
        rstd = carve([G])
        ssum = [carve([2 * H]) for _ in range(2)]
        norm = [carve([2 * H]) for _ in range(2)]
        rnorm = [carve([2 * H]) for _ in range(2)]
        ps_xt = banks[0:2]
        ps_qk = banks[2:4]
        ps_v = [banks[4][:, 0:D], banks[5][:, 0:D]]
        ps_pt = [banks[6][:, :].bitcast(bf16), banks[7][:, :].bitcast(bf16)]

        made = sem("made")
        w_in = sem("w_in")
        w_ps = sem("w_ps")
        w_sb = [sem(f"w_sb{i}") for i in range(2)]
        e_in = sem("e_in")
        b_in = sem("b_in")
        bias_ok = sem("bias_ok")
        b3_in = sem("b3_in")
        x_in = [sem(f"x_in{m}") for m in range(2)]
        x_used = sem("x_used")
        var_ok = sem("var_ok")
        sd_ok = sem("sd_ok")
        xn_ok = sem("xn_ok")
        xt_ps = sem("xt_ps")
        xt_ok = sem("xt_ok")
        qk_ps = sem("qk_ps")
        sq_ok = sem("sq_ok")
        ss_ok = sem("ss_ok")
        norm_ok = sem("norm_ok")
        v_ok = sem("v_ok")
        qn_ok = sem("qn_ok")
        hi_ok = sem("hi_ok")
        rest_ok = sem("rest_ok")
        mid_ok = sem("mid_ok")
        low_ok = sem("low_ok")
        pt0_ps = sem("pt0_ps")
        pt1_ps = sem("pt1_ps")
        pt0_ok = sem("pt0_ok")
        pt1_ok = sem("pt1_ok")
        parts_out = [sem(f"parts_out{m}") for m in range(2)]
        stack_in = sem("stack_in")
        dve_step = sem("dve_step")
        un_step = sem("un_step")

        def wait(engine, semaphore, value):
            if not isinstance(value, int) or value > 0:
                engine.wait_ge(semaphore, value)

        held = sem("held")

        def hold(engine, semaphore, value):
            engine.wait_ge(semaphore, value)
            engine.sem_inc(held, 1)

        TURNS = NG // 2
        NT = NG * G

        def real(k, j):
            return not isinstance(k, int) or 0 <= 2 * G * k + j < NT

        def weight_piece(i):
            bank = banks[i % 2]
            if i < 6:
                return w_t[:, :, i * P:(i + 1) * P], bank[:, 0:KC * P].rearrange("p (k n) -> p k n", k=KC)
            if i == 6:
                return wo_t[:, :, :], bank.rearrange("p (k n) -> p k n", k=KC)
            return cen_t[:, :, :], bank[:, 0:KC * NR].rearrange("p (k n) -> p k n", k=KC)

        def on(stage, k, j):
            if real(k, j):
                stage(k, j)

        def slots(engine, slot):
            for j in range(2 * G):
                slot(0, j)
            with engine.Fori(1, TURNS - 1) as k:
                for j in range(2 * G):
                    slot(k, j)
            for j in range(2 * G + 4):
                slot(TURNS - 1, j)

        def load_stacks(sp, k, h):
            head, buf = 2 * k + h, h % 2
            row = 0
            for part, times in ((0, 3), (1, 3), (2, 2)):
                for _ in range(times):
                    sp.dma_start(stacks[row:row + HD, 0, buf, :],
                                 qk_parts[0, part, bass.ds(head, 1), :, :].rearrange("o d s -> (o d) s")
                                 ).then_inc(stack_in, 16)
                    row += HD
            for row, n in ((0, 3), (3, 3), (6, 2)):
                sp.dma_start(stacks[row * HD:(row + n) * HD, 1, buf, :],
                             qk_parts[1, 0:n, bass.ds(head, 1), :, :].rearrange("p o d s -> (p o) d s")
                             ).then_inc(stack_in, 16)

        with nc.Block() as block:
            @block.gpsimd
            def _(pool):
                def load(g, m):
                    pool.dma_start(xin[m], x_rows[bass.ds(g * GT, GT), :].rearrange("(j p) d -> p j d", p=P)
                                   ).then_inc(x_in[m], 16)

                load(0, 0)
                load(1, 1)
                nc.gpsimd.memset(ident[:, :], 0.0).then_inc(made, 1)
                nc.gpsimd.memset(identb[:, :], 0.0).then_inc(made, 1)
                nc.gpsimd.memset(ones3[:, :], 1.0).then_inc(made, 1)
                nc.gpsimd.memset(one_c, 1.0).then_inc(made, 1)
                nc.gpsimd.memset(theta_c, 1.0 + PI / 2).then_inc(made, 1)
                nc.gpsimd.memset(eps_c, LN_EPS).then_inc(made, 1)
                nc.gpsimd.memset(vp[:, :, :], 0.0).then_inc(made, 1)
                pool.wait_ge(made, 7)
                for m in (ident, identb):
                    nc.gpsimd.affine_select(out=m[:, :], in_=m[:, :], compare_op=ALU.not_equal, fill=1.0,
                                            base=0, pattern=[[-1, P]], channel_multiplier=1).then_inc(made, 1)
                nc.gpsimd.memset(vp[:, :, 17:18], 1.0).then_inc(made, 1)
                for e in range(NR):
                    nc.gpsimd.memset(order[:, e:e + 1], float(NR - e)).then_inc(made, 1)
                nc.gpsimd.memset(gate2[:, :, NR:NX], 1.0 / NS).then_inc(made, 1)
                with pool.Fori(1, TURNS) as k:
                    for m in range(2):
                        hold(pool, x_used, (2 * k + m - 1) * G)
                        load(2 * k + m, m)

            @block.sync
            def _(sp):
                for m in range(2):
                    sp.sem_inc(parts_out[m], 1)
                sp.dma_start(w_nat, w_qkv.rearrange("(c p) d -> p c d", p=P)).then_inc(w_in, 16)
                for a, b, src in ((0, 3 * D, b_qkv), (3 * D, 4 * D, b_out), (4 * D, NBIAS, expert_biases)):
                    sp.dma_start(bias_row[:, a:b], src.rearrange("(a n) -> a n", a=1)).then_inc(b_in, 16)
                for dst, src in ((wo_nat, w_out.rearrange("(c p) d -> p c d", p=P)), (cen_nat, centroids),
                                 (be_rows[0:NR, :], br), (be_rows[NR:NX, :], bs)):
                    sp.dma_start(dst, src).then_inc(e_in, 16)
                sp.wait_ge(bias_ok, 5)
                for i in range(3):
                    sp.dma_start(bias3[i:i + 1, :], bias_part[i]).then_inc(b3_in, 16)

                def step(k, m):
                    hold(sp, pt0_ok, (2 * k + m) * G + G)
                    hold(sp, pt1_ok, (2 * k + m) * G + G)
                    for c in range(4):
                        for p in range(3):
                            dst = qk_parts[c // 2, p, bass.ds((k // (GPB // 2)) * H + c % 2 * 8, 8), :,
                                           bass.ds((k % (GPB // 2)) * 2 * GT + m * GT, GT)]
                            sp.dma_start(dst, parts_t[m][:, p * 4 + c, :]).then_inc(parts_out[m], 16)

                for m in range(2):
                    step(0, m)
                with sp.Fori(1, TURNS - 1) as k:
                    for m in range(2):
                        step(k, m)
                for h in range(2):
                    load_stacks(sp, 0, h)
                for m in range(2):
                    step(TURNS - 1, m)
                for m in range(2):
                    sp.wait_ge(parts_out[m], TURNS * 192 + 1)

            @block.scalar
            def _(act):
                for i in range(0, 8, 2):
                    act.wait_ge(w_ps, i + 1)
                    dst, src = weight_piece(i)
                    nc.scalar.activation(dst, src, ACT.Copy).then_inc(w_sb[0], 1)

                def deviations(k, m):
                    act.wait_ge(var_ok, (2 * k + m) * G + G)
                    nc.scalar.activation(sd, mv[:, :, 1], ACT.Sqrt, bias=eps_c).then_inc(sd_ok, 1)

                def copies(k, m):
                    g = 2 * k + m
                    for c in range(KC):
                        act.wait_ge(xt_ps, g * KC + c + 1)
                        if c == 0:
                            wait(act, qk_ps, (g - 1) * G)
                        nc.scalar.activation(xn_t[m % 2][:, c, :], ps_xt[c][:, :], ACT.Copy).then_inc(xt_ok, 1)

                def squares(k, j):
                    t = 2 * G * k + j
                    act.wait_ge(qk_ps, t + 1)
                    wait(act, ss_ok, t - 1)
                    nc.scalar.activation(sq[j % 2], ps_qk[j % 2], ACT.Square).then_inc(sq_ok, 1)
                    nc.scalar.activation(V[:, bass.ds((k // (GPB // 2)) * H, H),
                                           bass.ds((k % (GPB // 2)) * 2 * G + j, 1), :],
                                         ps_v[j % 2].rearrange("p (h o d) -> p h o d", h=H, o=1),
                                         ACT.Copy).then_inc(v_ok, 1)

                def norms(k, j):
                    act.wait_ge(ss_ok, 2 * G * k + j + 1)
                    nc.scalar.activation(norm[j % 2], ssum[j % 2], ACT.Sqrt).then_inc(norm_ok, 1)

                def high(k, j):
                    t = 2 * G * k + j
                    act.wait_ge(qn_ok, t + 1)
                    wait(act, pt1_ps, t - 3)
                    nc.scalar.activation(parts[j % 4][:, 0, :], qn[j % 2], ACT.Copy).then_inc(hi_ok, 1)

                def middle(k, j):
                    act.wait_ge(rest_ok, 2 * G * k + j + 1)
                    nc.scalar.activation(parts[j % 4][:, 1, :], rest[j % 2], ACT.Copy).then_inc(mid_ok, 1)

                def evacuate(k, j):
                    t = 2 * G * k + j
                    act.wait_ge(pt0_ps, t + 1)
                    if j % G == 0:
                        wait(act, parts_out[j // G % 2], (k + j // (2 * G)) * 192 + 1)
                    q = j % G * P
                    nc.scalar.activation(parts_t[j // G % 2][:, 0:8, q:q + P],
                                         ps_pt[0].rearrange("p (c n) -> p c n", c=8), ACT.Copy).then_inc(pt0_ok, 1)

                def slot(k, j):
                    on(evacuate, k, j - 4)
                    on(squares, k, j)
                    on(norms, k, j)
                    on(high, k, j - 1)
                    on(middle, k, j - 2)
                    if j % G == G - 1 and real(k, j + G + 1):
                        deviations(k, j // G + 2)
                    if j % G == 2 and real(k, j + G - 2):
                        copies(k, j // G + 1)

                deviations(0, 0)
                copies(0, 0)
                deviations(0, 1)
                slots(act, slot)

            @block.vector
            def _(dve):
                def statistics(k, m):
                    g = 2 * k + m
                    dve.wait_ge(x_in[m % 2], (k + m // 2) * 16 + 16)
                    for j in range(G):
                        nc.vector.bn_stats(stats[:, j, :], xin[m % 2][:, j, :]).then_inc(dve_step, 1)
                    hold(dve, dve_step, g * (G + 1) + G)
                    for j in range(G):
                        nc.vector.bn_aggr(mv[:, j, :], stats[:, j, :]).then_inc(var_ok, 1)

                def centre(k, m):
                    g = 2 * k + m
                    dve.wait_ge(sd_ok, g + 1)
                    nc.vector.reciprocal(rstd, sd).then_inc(dve_step, 1)
                    dve.wait_ge(dve_step, g * (G + 1) + G + 1)
                    wait(dve, xt_ps, (g - 1) * KC)
                    for j in range(G):
                        nc.vector.tensor_scalar(xn[m % 2][:, j, :], xin[m % 2][:, j, :], mv[:, j, 0:1],
                                                rstd[:, j:j + 1], ALU.subtract, ALU.mult).then_inc(x_used, 1)

                def sums(k, j):
                    t = 2 * G * k + j
                    dve.wait_ge(sq_ok, t + 1)
                    wait(dve, norm_ok, t - 1)
                    nc.vector.reduce_sum(ssum[j % 2], sq[j % 2].rearrange("p (h d) -> p h d", d=HD),
                                         AX.X).then_inc(ss_ok, 1)

                def unit(k, j):
                    t = 2 * G * k + j
                    dve.wait_ge(norm_ok, t + 1)
                    nc.vector.tensor_scalar_max(norm[j % 2], norm[j % 2], TINY).then_inc(un_step, 1)
                    dve.wait_ge(un_step, t * 2 + 1)
                    nc.vector.reciprocal(rnorm[j % 2], norm[j % 2]).then_inc(un_step, 1)
                    dve.wait_ge(un_step, t * 2 + 2)
                    wait(dve, hi_ok, t - 1)
                    nc.vector.tensor_tensor(qn[j % 2].rearrange("p (h d) -> p h d", d=HD),
                                            ps_qk[j % 2].rearrange("p (h d) -> p h d", d=HD),
                                            rnorm[j % 2].unsqueeze(2).broadcast_to([P, 2 * H, HD]),
                                            ALU.mult).then_inc(qn_ok, 1)

                def remainder(k, j):
                    t = 2 * G * k + j
                    dve.wait_ge(hi_ok, t + 1)
                    wait(dve, low_ok, t - 1)
                    nc.vector.tensor_tensor(rest[j % 2], qn[j % 2], parts[j % 4][:, 0, :],
                                            ALU.subtract).then_inc(rest_ok, 1)

                def low(k, j):
                    dve.wait_ge(mid_ok, 2 * G * k + j + 1)
                    nc.vector.tensor_tensor(parts[j % 4][:, 2, :], rest[j % 2], parts[j % 4][:, 1, :],
                                            ALU.subtract).then_inc(low_ok, 1)

                def evacuate(k, j):
                    dve.wait_ge(pt1_ps, 2 * G * k + j + 1)
                    if j % G == 0:
                        wait(dve, parts_out[j // G % 2], (k + j // (2 * G)) * 192 + 1)
                    q = j % G * P
                    nc.vector.tensor_copy(parts_t[j // G % 2][:, 8:12, q:q + P],
                                          ps_pt[1][:, 0:4 * P].rearrange("p (c n) -> p c n", c=4)
                                          ).then_inc(pt1_ok, 1)

                def slot(k, j):
                    on(evacuate, k, j - 4)
                    on(sums, k, j)
                    on(unit, k, j)
                    on(remainder, k, j - 1)
                    on(low, k, j - 2)
                    if j % G == 0 and real(k, j + G):
                        centre(k, j // G + 1)
                    if j % G == G - 2 and real(k, j + G + 2):
                        statistics(k, j // G + 2)

                dve.wait_ge(b_in, 48)
                for i in range(3):
                    nc.vector.tensor_copy(bias_part[i], bias_row).then_inc(bias_ok, 1)
                    dve.wait_ge(bias_ok, 2 * i + 1)
                    if i < 2:
                        nc.vector.tensor_tensor(bias_row, bias_row, bias_part[i], ALU.subtract).then_inc(bias_ok, 1)
                        dve.wait_ge(bias_ok, 2 * i + 2)
                for i in range(1, 8, 2):
                    dve.wait_ge(w_ps, i + 1)
                    dst, src = weight_piece(i)
                    nc.vector.tensor_copy(dst, src).then_inc(w_sb[1], 1)
                statistics(0, 0)
                centre(0, 0)
                statistics(0, 1)
                slots(dve, slot)

            @block.tensor
            def _(pe):
                pe.wait_ge(made, 11 + NR)
                pe.wait_ge(w_in, 16)
                for i in range(8):
                    if i >= 2:
                        pe.wait_ge(w_sb[i % 2], i // 2)
                    if i == 6:
                        pe.wait_ge(e_in, 4 * 16)
                    for kc in range(KC):
                        if i < 6:
                            last = nc.tensor.transpose(banks[i % 2][:, kc * P:(kc + 1) * P],
                                                       w_nat[:, i, kc * P:(kc + 1) * P], ident[:, :])
                        elif i == 6:
                            for oc in range(KC):
                                last = nc.tensor.transpose(banks[0][:, (kc * KC + oc) * P:(kc * KC + oc + 1) * P],
                                                           wo_nat[:, oc, kc * P:(kc + 1) * P], ident[:, :])
                        else:
                            last = nc.tensor.transpose(banks[1][:, kc * NR:(kc + 1) * NR],
                                                       cen_nat[:, kc * P:(kc + 1) * P], ident[0:NR, 0:NR])
                    last.then_inc(w_ps, 1)
                pe.wait_ge(b3_in, 48)
                pe.wait_ge(w_sb[0], 4)
                pe.wait_ge(w_sb[1], 4)

                def rows_t(k, m):
                    g = 2 * k + m
                    pe.wait_ge(x_used, g * G + G)
                    wait(pe, xt_ok, g * KC)
                    for c in range(KC):
                        for j in range(G):
                            last = nc.tensor.transpose(ps_xt[c][:, j * P:(j + 1) * P],
                                                       xn[m % 2][:, j, c * P:(c + 1) * P], ident[:, :])
                        last.then_inc(xt_ps, 1)

                def project(k, j):
                    t = 2 * G * k + j
                    if j % G == 0:
                        pe.wait_ge(xt_ok, (2 * k + j // G) * KC + KC)
                    wait(pe, qn_ok, t - 1)
                    wait(pe, v_ok, t - 1)
                    q = j % G * P
                    for dst, a, b in ((ps_qk[j % 2], 0, 2 * D), (ps_v[j % 2], 2 * D, 3 * D)):
                        for c in range(KC):
                            nc.tensor.matmul(dst, xn_t[j // G][:, c, q:q + P], w_t[:, c, a:b],
                                             start=(c == 0), stop=False)
                        mm = nc.tensor.matmul(dst, ones3[:, :], bias3[:, a:b], start=False, stop=True)
                    mm.then_inc(qk_ps, 1)

                def parts_rows(k, j):
                    t = 2 * G * k + j
                    pe.wait_ge(low_ok, t + 1)
                    for half, (ok, ps) in enumerate(((pt0_ok, pt0_ps), (pt1_ok, pt1_ps))):
                        wait(pe, ok, t)
                        for b in range(8 * half, 8 + 4 * half):
                            mm = nc.tensor.transpose(ps_pt[half][:, (b - 8 * half) * P:(b - 8 * half + 1) * P],
                                                     parts[j % 4][:, b // 4, b % 4 * P:(b % 4 + 1) * P],
                                                     identb[:, :])
                        mm.then_inc(ps, 1)

                def slot(k, j):
                    on(parts_rows, k, j - 4)
                    on(project, k, j)
                    if j % G == 2 and real(k, j + G - 2):
                        rows_t(k, j // G + 1)

                rows_t(0, 0)
                slots(pe, slot)

        nc.disable_value_cache = True
        ps_sum = banks[0]
        ps_clip = banks[1:3]
        ps_mult = banks[3:5]

        clip_ps = sem("clip_ps")
        clip_ok = sem("clip_ok")
        square_ok = sem("square_ok")
        log_ok = sem("log_ok")
        recip_ok = sem("recip_ok")
        mult_ps = sem("mult_ps")
        mult_ok = sem("mult_ok")
        atan_ok = sem("atan_ok")
        log2_ok = sem("log2_ok")
        score_ok = sem("score_ok")
        nc_ok = sem("nc_ok")
        vp_ok = sem("vp_ok")
        sum_ps = sem("sum_ps")
        sum_ok = sem("sum_ok")
        head_stored = sem("head_stored")
        LOADS = 11 * 16
        LAST = NB // 4 - 1
        SIDE = (LAST + 1) // 2
        assert B == 2 and LAST + 1 - SIDE == KT // 2
        room = V[:, 0:H, :, :].rearrange("p a b c -> p (a b c)")
        at[0] = 0
        we_t = [carve([KC, D if c == NC - 1 else 2 * D]) for c in range(NC)]
        assert at[0] <= BT * S
        w_ring = [room[:, i * 1024:(i + 1) * 1024].rearrange("p (k n) -> p k n", k=KC) for i in range(3)]
        side_den, side_nrow, side_scl = (room[0:4 * H, i * 512:(i + 1) * 512] for i in range(3))
        side_raw = room[:, 3072:3584].rearrange("p (c n) -> p c n", c=KC)
        side_scale = room[:, 3584:4096].rearrange("p (c n) -> p c n", c=KC)
        side_u = room[:, 3584:4096].rearrange("p (a d) -> p a d", a=2)
        ps_side = banks[5:7]
        ps_misc = banks[7]
        e_nat = rows2
        e_other = u2_t[:, :, :, :].rearrange("p h c n -> p (h c n)").rearrange("p (k n) -> p k n", k=KC)
        e_t = e_other
        cut = [0]

        def small(*dims):
            n = 2
            for d in dims:
                n *= d
            v = small2[:, cut[0]:cut[0] + n]
            cut[0] += n
            return v.rearrange("p (a d) -> p a d", a=2) if dims else v

        s_stat, s_mean = small(6), small(2)
        s_log, s_inv, s_tmp = small(), small(), small()
        s_top, s_sum, s_max = small(), small(), small()
        s_exp, s_eq, s_first, s_left = small(NR), small(NR), small(NR), small(NR)
        CH2 = 4

        en_in = sem("en_in")
        en_sum = sem("en_sum")
        et_ps = sem("et_ps")
        et_ok = sem("et_ok")
        et_out = sem("et_out")
        side_sums = sem("side_sums")
        side_scl_ok = sem("side_scl_ok")
        side_scl_out = sem("side_scl_out")
        side_in = sem("side_in")
        side_attn = sem("side_attn")
        side_y = sem("side_y")
        side_var = sem("side_var")
        side_inv = sem("side_inv")
        side_u_ok = sem("side_u_ok")
        side_u_ps = sem("side_u_ps")
        side_ut = sem("side_ut")
        side_l_ps = sem("side_l_ps")
        side_log = sem("side_log")
        side_l_ok = sem("side_l_ok")
        side_exp = sem("side_exp")
        side_gate = sem("side_gate")
        side_g_ps = sem("side_g_ps")
        side_gt = sem("side_gt")
        side_w = [sem(f"side_w{i}") for i in range(3)]
        side_e_ps = sem("side_e_ps")
        side_e_ok = sem("side_e_ok")
        side_out = sem("side_out")
        side_step = sem("side_step")
        t_in = sem("t_in")
        BEFORE, AFTER = (4, 5), (6, 7)
        RECIP_STARTS = (0, 1, 2, 4, 6)

        WEIGHTS = 1 + NR // 4
        assert NS == 2 and NR % 4 == 0 and WEIGHTS < SIDE

        def periods(engine, emit):
            for m in range(4):
                emit(0, m, "weights" if m == 3 else "")
            with engine.Fori(1, WEIGHTS) as k:
                for m in range(4):
                    emit(k, m, "weights")
            with engine.Fori(WEIGHTS, SIDE) as k:
                for m in range(4):
                    emit(k, m, "")
            for m in range(4):
                emit(SIDE, m, "tail")
            with engine.Fori(SIDE + 1, LAST) as k:
                for m in range(4):
                    emit(k, m, "tail")
            for m in range(4):
                emit(LAST, m, "tail")

        def expert(k, m):
            return 0 if isinstance(k, int) and k == 0 else 4 * (k - 1) + m + 1

        def has(k, m):
            return not (isinstance(k, int) and 4 * k + m >= NB)

        with nc.Block() as block:
            @block.sync
            def _(sp):
                def side_chunk(k, c):
                    if c >= 3 or not isinstance(k, int) or k > SIDE:
                        hold(sp, side_e_ok, (k - SIDE) * 2 * NE + (4 * (c - 2) if c >= 3 else (-6, -2, 0)[c]))
                    wide = D if c == NC - 1 else 2 * D
                    sp.dma_start(w_ring[c % 3][:, :, 0:wide], expert_w[c, :, :, 0:wide]).then_inc(side_w[c % 3], 16)

                def side_rows(k):
                    t2 = k - SIDE
                    if not isinstance(k, int) or k > SIDE:
                        hold(sp, side_u_ps, t2)
                        hold(sp, side_out, t2 * 16)
                    q = bass.ds((t2 % 2) * 2 * P, 2 * P)
                    for c in range(KC):
                        sp.dma_start(side_raw[:, c, :], head_out[c * 8:(c + 1) * 8, bass.ds(t2 // 2, 1), 0:HD, q].rearrange(
                            "h o r s -> (h o) r s")).then_inc(side_in, 16)
                        sp.dma_start(side_scale[:, c, :],
                                     row_scale[c * 8:(c + 1) * 8, bass.ds(t2 // 2, 1), q].broadcast_to(
                                         [8, HD, 2 * P])).then_inc(side_in, 16)
                    sp.dma_start(rows2[:, :, :], x_rows[bass.ds(t2 * 2 * P, 2 * P), :].rearrange(
                        "(j p) d -> p j d", p=P)).then_inc(side_in, 16)

                def side_before(k, m):
                    if m == 0 and isinstance(k, int) and k == SIDE:
                        sp.wait_ge(head_stored, H * 16)
                        sp.wait_ge(et_out, NE * 16)
                        for dst, r in ((side_den, HD), (side_nrow, HD + 1)):
                            sp.dma_start(dst, head_out[0:H, :, r, :].rearrange("h j s -> (h j) s")
                                         ).then_inc(side_sums, 16)
                        sp.wait_ge(side_scl_ok, 1)
                        sp.dma_start(row_scale[0:H, :, :].rearrange("h j s -> (h j) s"), side_scl
                                     ).then_inc(side_scl_out, 16)
                        sp.wait_ge(side_scl_out, 16)
                        for c in range(3):
                            side_chunk(k, c)
                    if m == 0:
                        side_rows(k)

                def side_after(k, m):
                    if m == 2:
                        for c in range(3, CH2 + 3):
                            side_chunk(k, c)
                    if m == 3:
                        for c in range(CH2 + 3, NC):
                            side_chunk(k, c)
                        if not (isinstance(k, int) and k == LAST):
                            for c in range(3):
                                side_chunk(k + 1, c)
                        hold(sp, side_e_ok, (k - SIDE + 1) * 2 * NE)
                        sp.dma_start(out_rows[bass.ds((k - SIDE) * 2 * P, 2 * P), :].rearrange(
                            "(j p) d -> p j d", p=P), rows2[:, :, :]).then_inc(side_out, 16)

                def emit(k, m, beside):
                    n = 4 * k + m
                    if beside == "tail":
                        side_before(k, m)
                    if beside == "weights":
                        if isinstance(k, int) and k == 0:
                            for e, dst in enumerate((e_nat[:, :, :], e_other)):
                                sp.dma_start(dst, Ws[e].rearrange("(c p) d -> p c d", p=P)).then_inc(en_in, 16)
                        else:
                            sp.dma_start(e_nat[:, :, :], Wr[bass.ds(4 * (k - 1) + m, 1), :, :].rearrange(
                                "o (c p) d -> p (o c) d", p=P)).then_inc(en_in, 16)
                    if isinstance(k, int) and n == NB - 1:
                        sp.wait_ge(sum_ps, (NB - 1) * BT)
                        for c in range(NC):
                            sp.dma_start(we_t[c], expert_w[c, :, :, 0:D if c == NC - 1 else 2 * D]).then_inc(t_in, 16)
                    if m % 2 == 0:
                        if has(k, m + 4):
                            hold(sp, mult_ok, (n + 2) * 4 * BT)
                            load_stacks(sp, k, m // 2 + 2)
                    else:
                        head = 2 * k + m // 2
                        hold(sp, sum_ok, head + 1)
                        sp.dma_start(head_out[bass.ds(head, 1)].rearrange("o j r s -> (o j r) s"),
                                     evac[:, :]).then_inc(head_stored, 16)
                    if beside == "weights":
                        hold(sp, et_ok, expert(k, m) + 1)
                        if isinstance(k, int) and k == 0:
                            dst = expert_w[NC - 1, :, :, 0:D]
                        else:
                            dst = expert_w[bass.ds(2 * (k - 1) + m // 2, 1), :, :, m % 2 * D:(m % 2 + 1) * D].rearrange(
                                "o p k n -> (o p) k n")
                        sp.dma_start(dst, e_t).then_inc(et_out, 16)
                    if beside == "tail":
                        side_after(k, m)

                periods(sp, emit)
                sp.wait_ge(head_stored, NH * 16)
                sp.wait_ge(side_out, KT // 2 * 16)

            @block.tensor
            def _(pe):
                def cosines(dst, m, i, q0, n):
                    buf = m // 2 % 2
                    keys = (m % 2 * BT + i) * P
                    return nc.tensor.matmul(dst, stacks[:, 1, buf, keys:keys + P],
                                            stacks[:, 0, buf, q0:q0 + n], start=True, stop=True)

                def clip(k, m, i):
                    for j in range(4):
                        wait(pe, clip_ok, ((4 * k + m) * BT + i) * 4 + j - 1)
                        cosines(ps_clip[j % 2], m, i, j * 512, 512).then_inc(clip_ps, 1)

                def mult(k, m, i):
                    for j in range(4):
                        wait(pe, mult_ok, ((4 * k + m) * BT + i) * 4 + j - 1)
                        cosines(ps_mult[j % 2], m, i, j * 512, 512).then_inc(mult_ps, 1)

                def add(k, m, i):
                    t = (4 * k + m) * BT + i
                    pe.wait_ge(vp_ok, t + 1)
                    if m % 2 == 0 and i == 0:
                        wait(pe, sum_ok, 2 * k + m // 2)
                    for j in range(4):
                        mm = nc.tensor.matmul(ps_sum[32 * j:32 * j + 32, :], vp[:, i % 4, :],
                                              X[:, m % 2, i, j * 512:(j + 1) * 512],
                                              start=(m % 2 == 0 and i == 0), stop=(m % 2 == 1 and i == BT - 1),
                                              tile_position=(0, 32 * j))
                    mm.then_inc(sum_ps, 1)

                def side_chunks(k, a, b):
                    for c in range(a, b):
                        pe.wait_ge(side_w[c % 3], ((k - SIDE) * 3 + c // 3 + 1) * 16)
                        wide = D if c == NC - 1 else 2 * D
                        for h in range(2):
                            wait(pe, side_e_ok, (k - SIDE) * 2 * NE + (4 * c + 2 * h - 2 if c else h - 1))
                            dst = ps_side[h][:, 0:wide]
                            for kc in range(KC):
                                mm = nc.tensor.matmul(dst, u2_t[:, h, kc, :], w_ring[c % 3][:, kc, 0:wide],
                                                      start=(kc == 0), stop=(kc == KC - 1 and wide == 2 * D))
                            if wide == D:
                                mm = nc.tensor.matmul(dst, gate2_t[:, h, :], be_rows[:, :], start=False, stop=True)
                            mm.then_inc(side_e_ps, 1)

                def side_work(k, m):
                    t2 = k - SIDE
                    if m == 0:
                        pe.wait_ge(side_attn, t2 + 1)
                        for h in range(2):
                            dst = ps_misc[:, h * D:(h + 1) * D]
                            for c in range(KC):
                                nc.tensor.matmul(dst, side_raw[:, c, h * P:(h + 1) * P], wo_t[:, c, :],
                                                 start=(c == 0), stop=False)
                            mm = nc.tensor.matmul(dst, ones3[:, :], bias3[:, 3 * D:4 * D], start=False, stop=True)
                        mm.then_inc(side_y, 1)
                    if m == 1:
                        pe.wait_ge(side_u_ok, (t2 + 1) * 2)
                        for h in range(2):
                            for c in range(KC):
                                mm = nc.tensor.transpose(ps_misc[:, (h * KC + c) * P:(h * KC + c + 1) * P],
                                                         side_u[:, h, c * P:(c + 1) * P], ident[:, :])
                        mm.then_inc(side_u_ps, 1)
                        pe.wait_ge(side_ut, t2 + 1)
                        for h in range(2):
                            dst = ps_misc[:, h * NR:(h + 1) * NR]
                            for c in range(KC):
                                nc.tensor.matmul(dst, u2_t[:, h, c, :], cen_t[:, c, :], start=(c == 0), stop=False)
                            mm = nc.tensor.matmul(dst, ones3[:, :], bias3[:, 4 * D:NBIAS], start=False, stop=True)
                        mm.then_inc(side_l_ps, 1)
                    if m == 2:
                        pe.wait_ge(side_gate, t2 + 1)
                        for h in range(2):
                            mm = nc.tensor.transpose(ps_misc[0:NX, h * P:(h + 1) * P], gate2[:, h, :], ident[:, :])
                        mm.then_inc(side_g_ps, 1)
                        side_chunks(k, 0, CH2)
                    if m == 3:
                        pe.wait_ge(side_gt, t2 + 1)
                        side_chunks(k, CH2, NC)

                def emit(k, m, beside):
                    if m % 2 == 0 and has(k, m + 2):
                        pe.wait_ge(stack_in, (2 * k + m // 2 + 2) * LOADS)
                    for i in range(BT // 2):
                        if has(k, m + 2):
                            clip(k, m + 2, i)
                        add(k, m, 2 * i)
                        add(k, m, 2 * i + 1)
                    if has(k, m + 2):
                        for i in BEFORE:
                            clip(k, m + 2, i)
                    if has(k, m + 1):
                        for i in range(BT):
                            mult(k, m + 1, i)
                    if has(k, m + 2):
                        for i in AFTER:
                            clip(k, m + 2, i)
                    if beside == "weights":
                        if isinstance(k, int) and k == 0:
                            pe.wait_ge(en_sum, 1)
                        else:
                            pe.wait_ge(en_in, (expert(k, m) + 2) * 16)
                        for kc in range(KC):
                            for oc in range(KC):
                                mm = nc.tensor.transpose(ps_misc[:, (kc * KC + oc) * P:(kc * KC + oc + 1) * P],
                                                         e_nat[:, oc, kc * P:(kc + 1) * P], ident[:, :])
                        mm.then_inc(et_ps, 1)
                    if beside == "tail":
                        side_work(k, m)

                pe.wait_ge(stack_in, 2 * LOADS)
                for i in range(BT):
                    clip(0, 0, i)
                for i in range(BT // 2):
                    clip(0, 1, i)
                for i in range(BT):
                    mult(0, 0, i)
                    if i % 2:
                        clip(0, 1, BT // 2 + i // 2)
                periods(pe, emit)

            @block.vector
            def _(dve):
                def clip(k, m, i):
                    t = (4 * k + m) * BT + i
                    wait(dve, square_ok, t - 1)
                    for j in range(4):
                        dve.wait_ge(clip_ps, t * 4 + j + 1)
                        nc.vector.tensor_scalar(cosc[:, i % 2, j * 512:(j + 1) * 512], ps_clip[j % 2],
                                                -CLIP, CLIP, ALU.max, ALU.min).then_inc(clip_ok, 1)

                def mult(k, m, i):
                    t = (4 * k + m) * BT + i
                    if i in RECIP_STARTS:
                        dve.wait_ge(recip_ok, (4 * k + m) * len(RECIP_STARTS) + RECIP_STARTS.index(i) + 1)
                    for j in range(4):
                        dve.wait_ge(mult_ps, t * 4 + j + 1)
                        part = X[:, m % 2, i, j * 512:(j + 1) * 512]
                        nc.vector.tensor_tensor(part, ps_mult[j % 2], part, ALU.mult).then_inc(mult_ok, 1)

                def values(k, m, i):
                    t = (4 * k + m) * BT + i
                    dve.wait_ge(score_ok, t + 1)
                    wait(dve, sum_ps, t - 3)
                    nc.vector.reciprocal(vp[:, i % 4, HD:HD + 1], ncol[:, i:i + 1]).then_inc(nc_ok, 1)
                    dve.wait_ge(nc_ok, t + 1)
                    nc.vector.tensor_scalar(vp[:, i % 4, 0:HD],
                                            V[:, bass.ds(2 * k + m // 2, 1), m % 2 * BT + i, :].rearrange(
                                                "p o d -> p (o d)"),
                                            vp[:, i % 4, HD:HD + 1], None, ALU.mult).then_inc(vp_ok, 1)

                SCALE_STEPS, PAIR_STEPS = 4, 24
                steps = [0]

                def link(ins):
                    steps[0] = steps[0] + 1
                    ins.then_inc(side_step, 1)
                    dve.wait_ge(side_step, steps[0])

                def side_scales():
                    dve.wait_ge(side_sums, 32)
                    link(nc.vector.reciprocal(side_nrow, side_nrow))
                    link(nc.vector.tensor_tensor(side_den, side_den, side_nrow, ALU.mult))
                    link(nc.vector.tensor_scalar_max(side_den, side_den, TINY))
                    link(nc.vector.reciprocal(side_den, side_den))
                    nc.vector.tensor_tensor(side_scl, side_den, side_nrow, ALU.mult).then_inc(side_scl_ok, 1)

                def side_residual(k):
                    t2 = k - SIDE
                    dve.wait_ge(side_in, (t2 + 1) * 80)
                    nc.vector.tensor_tensor(side_raw, side_raw, side_scale, ALU.mult).then_inc(side_attn, 1)
                    dve.wait_ge(side_y, t2 + 1)
                    link(nc.vector.tensor_tensor(rows2[:, :, :], ps_misc.rearrange("p (a d) -> p a d", a=2),
                                                 rows2[:, :, :], ALU.add))
                    for h in range(2):
                        steps[0] = steps[0] + 1
                        nc.vector.bn_stats(s_stat[:, h, :], rows2[:, h, :]).then_inc(side_step, 1)
                    hold(dve, side_step, steps[0])
                    for h in range(2):
                        nc.vector.bn_aggr(s_mean[:, h, :], s_stat[:, h, :]).then_inc(side_var, 1)

                def side_normal(k):
                    t2 = k - SIDE
                    dve.wait_ge(side_inv, t2 + 1)
                    link(nc.vector.tensor_tensor(s_tmp, s_inv, s_inv, ALU.mult))
                    link(nc.vector.scalar_tensor_tensor(s_tmp, s_mean[:, :, 1], LN_EPS, s_tmp, ALU.add, ALU.mult))
                    link(nc.vector.tensor_scalar(s_tmp, s_tmp, -0.5, 1.5, ALU.mult, ALU.add))
                    link(nc.vector.tensor_tensor(s_inv, s_inv, s_tmp, ALU.mult))
                    for h in range(2):
                        nc.vector.tensor_scalar(side_u[:, h, :], rows2[:, h, :], s_mean[:, h, 0:1],
                                                s_inv[:, h:h + 1], ALU.subtract, ALU.mult).then_inc(side_u_ok, 1)
                    dve.wait_ge(side_u_ok, (t2 + 1) * 2)
                    link(nc.vector.tensor_tensor(rows2[:, :, :], rows2[:, :, :], side_u, ALU.add))
                    dve.wait_ge(side_u_ps, t2 + 1)
                    nc.vector.tensor_copy(u2_t[:, :, :, :], ps_misc.rearrange("p (h c n) -> p h c n", h=2, c=KC)
                                          ).then_inc(side_ut, 1)
                    dve.wait_ge(side_l_ps, t2 + 1)
                    logits = ps_misc[:, 0:2 * NR].rearrange("p (h e) -> p h e", h=2)
                    link(nc.vector.reduce_max(s_top, logits, AX.X))
                    nc.vector.tensor_tensor(s_exp, logits, spread(s_top), ALU.subtract).then_inc(side_l_ok, 1)

                def spread(v):
                    return v.unsqueeze(2).broadcast_to([P, 2, NR])

                def side_choose(k):
                    t2 = k - SIDE
                    ranks = order[:, :].unsqueeze(1).broadcast_to([P, 2, NR])
                    dve.wait_ge(side_exp, t2 + 1)
                    link(nc.vector.reduce_sum(s_sum, s_exp, AX.X))
                    link(nc.vector.reciprocal(s_sum, s_sum))
                    link(nc.vector.tensor_tensor(s_exp, s_exp, spread(s_sum), ALU.mult))
                    for own, chosen in ((s_exp, s_first), (s_left, s_eq)):
                        link(nc.vector.reduce_max(s_max, own, AX.X))
                        link(nc.vector.tensor_tensor(s_eq, own, spread(s_max), ALU.is_equal))
                        link(nc.vector.tensor_tensor(s_eq, s_eq, ranks, ALU.mult))
                        link(nc.vector.reduce_max(s_max, s_eq, AX.X))
                        link(nc.vector.tensor_tensor(chosen, s_eq, spread(s_max), ALU.is_equal))
                        if own is s_exp:
                            link(nc.vector.scalar_tensor_tensor(s_left, s_first, -2.0, s_exp, ALU.mult, ALU.add))
                    link(nc.vector.tensor_tensor(s_first, s_first, s_eq, ALU.add))
                    nc.vector.tensor_tensor(gate2[:, :, 0:NR], s_exp, s_first, ALU.mult).then_inc(side_gate, 1)
                    dve.wait_ge(side_g_ps, t2 + 1)
                    nc.vector.tensor_copy(gate2_t[:, :, :], ps_misc[0:NX, 0:2 * P].rearrange("p (h n) -> p h n", h=2)
                                          ).then_inc(side_gt, 1)

                def side_gather(k, a, b):
                    t2 = k - SIDE
                    for c in range(a, b):
                        for h in range(2):
                            dve.wait_ge(side_e_ps, t2 * 2 * NC + 2 * c + h + 1)
                            if c == NC - 1:
                                nc.vector.tensor_tensor(rows2[:, h, :], ps_side[h][:, 0:D], rows2[:, h, :],
                                                        ALU.add).then_inc(side_e_ok, 1)
                                continue
                            for e in (2 * c, 2 * c + 1):
                                nc.vector.scalar_tensor_tensor(rows2[:, h, :], ps_side[h][:, e % 2 * D:(e % 2 + 1) * D],
                                                               gate2[:, h, e:e + 1], rows2[:, h, :],
                                                               ALU.mult, ALU.add).then_inc(side_e_ok, 1)
                                dve.wait_ge(side_e_ok, t2 * 2 * NE + 4 * c + 2 * h + e % 2 + 1)

                def side_work(k, m):
                    if m == 0:
                        side_residual(k)
                    if m == 1:
                        side_normal(k)
                    if m == 2:
                        side_choose(k)
                        side_gather(k, 0, CH2)
                    if m == 3:
                        side_gather(k, CH2, NC)

                def emit(k, m, beside):
                    for i in range(BT // 2):
                        values(k, m, 2 * i)
                        values(k, m, 2 * i + 1)
                        if has(k, m + 2):
                            clip(k, m + 2, i)
                    if has(k, m + 2):
                        for i in BEFORE:
                            clip(k, m + 2, i)
                    if has(k, m + 1):
                        for i in range(BT):
                            mult(k, m + 1, i)
                    if beside == "tail" and isinstance(k, int) and k == SIDE and m == 0:
                        side_scales()
                        assert steps[0] == SCALE_STEPS
                    if has(k, m + 2):
                        for i in AFTER:
                            clip(k, m + 2, i)
                    if m % 2 == 1:
                        head = 2 * k + m // 2
                        dve.wait_ge(sum_ps, (head + 1) * KT)
                        wait(dve, head_stored, head * 16)
                        nc.vector.tensor_copy(evac[:, :], ps_sum).then_inc(sum_ok, 1)
                    if beside == "weights":
                        shared = isinstance(k, int) and k == 0
                        if shared:
                            dve.wait_ge(en_in, 32)
                            nc.vector.tensor_tensor(e_nat[:, :, :], e_nat[:, :, :], e_other, ALU.add).then_inc(en_sum, 1)
                        dve.wait_ge(et_ps, expert(k, m) + 1)
                        wait(dve, et_out, expert(k, m) * 16)
                        nc.vector.tensor_scalar(e_t, ps_misc.rearrange("p (k n) -> p k n", k=KC),
                                                1.0 / NS if shared else 1.0, None, ALU.mult).then_inc(et_ok, 1)
                    if beside == "tail":
                        if m == 0 and not (isinstance(k, int) and k == SIDE):
                            steps[0] = SCALE_STEPS + (k - SIDE) * PAIR_STEPS
                        side_work(k, m)
                        if m == 3 and isinstance(k, int) and k == SIDE:
                            assert steps[0] == SCALE_STEPS + PAIR_STEPS

                for i in range(BT):
                    clip(0, 0, i)
                for i in range(BT // 2):
                    clip(0, 1, i)
                for i in range(BT):
                    mult(0, 0, i)
                    if i % 2:
                        clip(0, 1, BT // 2 + i // 2)
                periods(dve, emit)

            @block.gpsimd
            def _(pool):
                def square(k, m, i):
                    t = (4 * k + m) * BT + i
                    pool.wait_ge(clip_ok, t * 4 + 4)
                    wait(pool, sum_ps, t - 2 * BT + 1)
                    nc.gpsimd.tensor_tensor(X[:, m % 2, i, :], cosc[:, i % 2, :], cosc[:, i % 2, :],
                                            ALU.mult).then_inc(square_ok, 1)

                def emit(k, m, beside):
                    if has(k, m + 2):
                        for i in range(BT):
                            square(k, m + 2, i)

                hold(pool, square_ok, BT)
                for i in range(BT):
                    square(0, 1, i)
                periods(pool, emit)

            @block.scalar
            def _(act):
                def tiles(m, a, b):
                    return X[:, m % 2, a:b, :]

                def sines(k, m):
                    n = 4 * k + m
                    act.wait_ge(square_ok, n * BT + BT)
                    own = tiles(m, 0, BT)
                    nc.scalar.activation(own, own, ACT.Ln, bias=one_c, scale=-1.0).then_inc(log_ok, 1)
                    for a, b in zip(RECIP_STARTS, RECIP_STARTS[1:] + (BT,)):
                        act.wait_ge(log_ok, n + 1)
                        own = tiles(m, a, b)
                        nc.scalar.activation(own, own, ACT.Sigmoid, scale=-0.5).then_inc(recip_ok, 1)
                    for a, b in ((0, 4), (4, 6), (6, 8)):
                        act.wait_ge(mult_ok, (n * BT + b) * 4)
                        own = tiles(m, a, b)
                        nc.scalar.activation(own, own, ACT.Arctan).then_inc(atan_ok, 1)

                def scores(k, m):
                    n = 4 * k + m
                    nc.scalar.preload_act_table_set("natural_log_exp_and_others")
                    act.wait_ge(atan_ok, n * 3 + 3)
                    own = tiles(m, 0, BT)
                    nc.scalar.activation(own, own, ACT.Ln, bias=theta_c, scale=-2.0).then_inc(log2_ok, 1)
                    for i in range(BT):
                        act.wait_ge(log2_ok, n + 1)
                        nc.scalar.activation(X[:, m % 2, i, :], X[:, m % 2, i, :], ACT.Exp, scale=POWER,
                                             accum_out=ncol[:, i:i + 1]).then_inc(score_ok, 1)

                def emit(k, m, beside):
                    scores(k, m)
                    if beside == "tail" and m == 1:
                        act.wait_ge(side_var, (k - SIDE + 1) * 2)
                        nc.scalar.activation(s_log, s_mean[:, :, 1], ACT.Ln, bias=eps_c).then_inc(side_log, 1)
                        act.wait_ge(side_log, k - SIDE + 1)
                        nc.scalar.activation(s_inv, s_log, ACT.Exp, scale=-0.5).then_inc(side_inv, 1)
                    if beside == "tail" and m == 2:
                        act.wait_ge(side_l_ok, k - SIDE + 1)
                        nc.scalar.activation(s_exp, s_exp, ACT.Exp).then_inc(side_exp, 1)
                    if has(k, m + 1):
                        sines(k, m + 1)

                for i in range(BT):
                    act.wait_ge(clip_ok, i * 4 + 4)
                    nc.scalar.activation(X[:, 0, i, :], cosc[:, i % 2, :], ACT.Square).then_inc(square_ok, 1)
                sines(0, 0)
                periods(act, emit)

        at[0] = (KC * NC * 2 - KC) * D
        den = carve([256])
        nrow = carve([256])
        scl = carve([256])
        raw = carve([KC, GT])
        scale_b = carve([KC, GT])
        attn = carve([KC, GT])
        xres = carve([G, D])
        x1 = carve([D])
        u = carve([D])
        acc = [carve([2, D]) for _ in range(2)]
        STEPS = NE + 1
        u_t = [carve([KC, P]) for _ in range(2)]
        gate = [carve([NX]) for _ in range(2)]
        gate_t = [carve([P], parts=NX) for _ in range(2)]
        stat = carve([6])
        mean = carve([2])
        dev = carve([1])
        rdev = carve([1])
        top = carve([1])
        neg_top = carve([1])
        expd = carve([NR])
        esum = carve([1])
        resum = carve([1])
        prob = carve([NR])
        m1 = carve([1])
        t1 = carve([NR])
        w1 = carve([1])
        f1 = carve([NR])
        p2 = carve([NR])
        m2 = carve([1])
        t2 = carve([NR])
        w2 = carve([1])
        f2 = carve([NR])
        ps_e = banks[0:3]
        ps_y, ps_u, ps_l, ps_g = banks[3], banks[4], banks[5], banks[6]
        ps_l = ps_l[:, 0:NR]

        t_sums = sem("t_sums")
        t_made = sem("t_made")
        scale_ok = sem("scale_ok")
        scale_out = sem("scale_out")
        raw_in = sem("raw_in")
        xres_in = sem("xres_in")
        attn_ok = sem("attn_ok")
        y_ps = sem("y_ps")
        x1_ok = sem("x1_ok")
        var2_ok = sem("var2_ok")
        dev_ok = sem("dev_ok")
        u_ok = sem("u_ok")
        u_ps = sem("u_ps")
        ut_ok = sem("ut_ok")
        l_ps = sem("l_ps")
        top_ok = sem("top_ok")
        exp_ok = sem("exp_ok")
        gate_ok = sem("gate_ok")
        g_ps = sem("g_ps")
        gt_ok = sem("gt_ok")
        e_ps = sem("e_ps")
        e_ok = sem("e_ok")
        rows_out = sem("rows_out")
        chain3 = sem("chain3")

        def blocks(engine, emit):
            emit(0)
            with engine.Fori(1, GPB - 1) as k:
                emit(k)
            emit(GPB - 1)

        def final(k, j):
            return isinstance(k, int) and k == GPB - 1 and j == G - 1

        with nc.Block() as block:
            @block.gpsimd
            def _(pool):
                for g in gate:
                    nc.gpsimd.memset(g[:, NR:NX], 1.0 / NS).then_inc(t_made, 1)

            @block.sync
            def _(sp):
                halves = [(slice(a * 4 * H, (a + 1) * 4 * H), slice(a * 256, (a + 1) * 256)) for a in range(2)]
                for dst, r in ((den, HD), (nrow, HD + 1)):
                    for own, q in halves:
                        sp.dma_start(dst[own, :], head_out[H:NH, :, r, q].rearrange("h j s -> (h j) s")
                                     ).then_inc(t_sums, 16)

                def load_sums(k):
                    for c in range(KC):
                        sp.dma_start(raw[:, c, :], head_out[H + c * 8:H + c * 8 + 8, bass.ds(k, 1), 0:HD, :].rearrange(
                            "h o r s -> (h o) r s")).then_inc(raw_in, 16)

                def load_scales(k):
                    for c in range(KC):
                        sp.dma_start(scale_b[:, c, :], row_scale[H + c * 8:H + c * 8 + 8, bass.ds(k, 1), :].broadcast_to(
                            [8, HD, 512])).then_inc(raw_in, 16)

                def load_x(k):
                    sp.dma_start(xres, x_rows[bass.ds((k + GPB) * GT, GT), :].rearrange("(j p) d -> p j d", p=P)
                                 ).then_inc(xres_in, 16)

                load_sums(0)
                load_x(0)
                sp.wait_ge(scale_ok, 1)
                for own, q in halves:
                    sp.dma_start(row_scale[H:NH, :, q].rearrange("h j s -> (h j) s"), scl[own, :]
                                 ).then_inc(scale_out, 16)
                sp.wait_ge(scale_out, 32)

                def store(k, j):
                    hold(sp, e_ok, (k * G + j + 1) * STEPS)
                    sp.dma_start(out_rows[bass.ds(((k + GPB) * G + j) * P, P), :], acc[j % 2][:, 0, :]).then_inc(rows_out, 16)
                    hold(sp, rows_out, (k * G + j + 1) * 16)

                def emit(k):
                    last = isinstance(k, int) and k == GPB - 1
                    if not last:
                        hold(sp, attn_ok, k * G + G)
                        load_sums(k + 1)
                        load_scales(k + 1)
                    for j in range(G):
                        if j == G - 2 and not last:
                            hold(sp, x1_ok, (k + 1) * G)
                            load_x(k + 1)
                        store(k, j)

                load_scales(0)
                blocks(sp, emit)

            @block.tensor
            def _(pe):
                pe.wait_ge(t_in, NC * 16)
                pe.wait_ge(t_made, 2)

                def y(k, j):
                    t = k * G + j
                    pe.wait_ge(attn_ok, t + 1)
                    wait(pe, x1_ok, t)
                    for c in range(KC):
                        nc.tensor.matmul(ps_y[:, 0:D], attn[:, c, j * P:(j + 1) * P], wo_t[:, c, :],
                                         start=(c == 0), stop=False)
                    nc.tensor.matmul(ps_y[:, 0:D], ones3[:, :], bias3[:, 3 * D:4 * D], start=False,
                                     stop=True).then_inc(y_ps, 1)

                def u_rows(k, j):
                    t = k * G + j
                    pe.wait_ge(u_ok, t + 1)
                    wait(pe, ut_ok, t)
                    for c in range(KC):
                        mm = nc.tensor.transpose(ps_u[:, c * P:(c + 1) * P], u[:, c * P:(c + 1) * P], ident[:, :])
                    mm.then_inc(u_ps, 1)

                def logits(k, j):
                    t = k * G + j
                    pe.wait_ge(ut_ok, t + 1)
                    wait(pe, exp_ok, t)
                    for c in range(KC):
                        nc.tensor.matmul(ps_l, u_t[j % 2][:, c, :], cen_t[:, c, :], start=(c == 0), stop=False)
                    nc.tensor.matmul(ps_l, ones3[:, :], bias3[:, 4 * D:NBIAS], start=False, stop=True).then_inc(l_ps, 1)

                def gates(k, j):
                    t = k * G + j
                    pe.wait_ge(gate_ok, t + 1)
                    wait(pe, gt_ok, t)
                    nc.tensor.transpose(ps_g[0:NX, 0:P], gate[j % 2], ident[:, :]).then_inc(g_ps, 1)

                def experts(k, j, c):
                    wait(pe, e_ok, (k * G + j) * STEPS + (-4, -2, -1, 2, 4, 6, 8, 10, 12)[c])
                    wide = 2 * D if c < NR // 2 else D
                    dst = ps_e[c % 3][:, 0:wide]
                    for kc in range(KC):
                        mm = nc.tensor.matmul(dst, u_t[j % 2][:, kc, :], we_t[c][:, kc, :],
                                              start=(kc == 0), stop=(kc == KC - 1 and wide == 2 * D))
                    if wide == D:
                        pe.wait_ge(gt_ok, k * G + j + 1)
                        mm = nc.tensor.matmul(dst, gate_t[j % 2], be_rows[:, :], start=False, stop=True)
                    mm.then_inc(e_ps, 1)

                y(0, 0)
                u_rows(0, 0)
                logits(0, 0)
                gates(0, 0)

                def emit(k):
                    for j in range(G):
                        nk, nj = (k, j + 1) if j < G - 1 else (k + 1, 0)
                        more = not final(k, j)
                        if more:
                            y(nk, nj)
                        for c in range(3):
                            experts(k, j, c)
                        if more:
                            u_rows(nk, nj)
                        for c in range(3, 5):
                            experts(k, j, c)
                        if more:
                            logits(nk, nj)
                        for c in range(5, 9):
                            experts(k, j, c)
                        if more:
                            gates(nk, nj)

                blocks(pe, emit)

            @block.scalar
            def _(act):
                def sd3(k, j):
                    act.wait_ge(var2_ok, k * G + j + 1)
                    nc.scalar.activation(dev, mean[:, 1:2], ACT.Sqrt, bias=eps_c).then_inc(dev_ok, 1)

                def ut(k, j):
                    t = k * G + j
                    act.wait_ge(u_ps, t + 1)
                    wait(act, e_ps, (t - 1) * 9)
                    nc.scalar.activation(u_t[j % 2], ps_u[:, 0:D].rearrange("p (k n) -> p k n", k=KC),
                                         ACT.Copy).then_inc(ut_ok, 1)

                def exps(k, j):
                    act.wait_ge(top_ok, k * G + j + 1)
                    nc.scalar.activation(expd, ps_l, ACT.Exp, bias=neg_top, accum_out=esum).then_inc(exp_ok, 1)

                def gt(k, j):
                    act.wait_ge(g_ps, k * G + j + 1)
                    nc.scalar.activation(gate_t[j % 2], ps_g[0:NX, 0:P], ACT.Copy).then_inc(gt_ok, 1)

                def tile(k, j):
                    sd3(k, j)
                    ut(k, j)
                    exps(k, j)
                    gt(k, j)

                def emit(k):
                    for j in range(G):
                        if not final(k, j):
                            tile(*((k, j + 1) if j < G - 1 else (k + 1, 0)))

                tile(0, 0)
                blocks(act, emit)

            @block.vector
            def _(dve):
                count = [0]

                def link(ins):
                    count[0] = count[0] + 1
                    ins.then_inc(chain3, 1)
                    dve.wait_ge(chain3, count[0])

                dve.wait_ge(t_sums, 64)
                link(nc.vector.reciprocal(nrow, nrow))
                link(nc.vector.tensor_tensor(den, den, nrow, ALU.mult))
                link(nc.vector.tensor_scalar_max(den, den, TINY))
                link(nc.vector.reciprocal(den, den))
                nc.vector.tensor_tensor(scl, den, nrow, ALU.mult).then_inc(scale_ok, 1)

                def scaled(k, j):
                    if j == 0:
                        dve.wait_ge(raw_in, (k + 1) * 4 * 16)
                    wait(dve, y_ps, (k - 1) * G + j + 1)
                    q = slice(j * P, (j + 1) * P)
                    nc.vector.tensor_tensor(attn[:, :, q], raw[:, :, q], scale_b[:, :, q],
                                            ALU.mult).then_inc(attn_ok, 1)

                def residual(k, j):
                    t = k * G + j
                    if j == 0:
                        dve.wait_ge(xres_in, (k + 1) * 16)
                    dve.wait_ge(y_ps, t + 1)
                    nc.vector.tensor_tensor(x1, ps_y[:, 0:D], xres[:, j, :], ALU.add).then_inc(x1_ok, 1)
                    dve.wait_ge(x1_ok, t + 1)
                    link(nc.vector.bn_stats(stat, x1))
                    dve.sem_inc(held, 1)
                    nc.vector.bn_aggr(mean, stat).then_inc(var2_ok, 1)

                def centred(k, j):
                    t = k * G + j
                    dve.wait_ge(dev_ok, t + 1)
                    link(nc.vector.reciprocal(rdev, dev))
                    wait(dve, u_ps, t)
                    nc.vector.tensor_scalar(u, x1, mean[:, 0:1], rdev, ALU.subtract, ALU.mult).then_inc(u_ok, 1)
                    dve.wait_ge(u_ok, t + 1)
                    wait(dve, rows_out, (t - 1) * 16)
                    link(nc.vector.tensor_tensor(acc[j % 2][:, 0, :], x1, u, ALU.add))

                def highest(k, j):
                    dve.wait_ge(l_ps, k * G + j + 1)
                    link(nc.vector.reduce_max(top, ps_l, AX.X))
                    nc.vector.tensor_scalar(neg_top, top, -1.0, None, ALU.mult).then_inc(top_ok, 1)

                def choose(k, j):
                    t = k * G + j
                    dve.wait_ge(exp_ok, t + 1)
                    link(nc.vector.reciprocal(resum, esum))
                    link(nc.vector.tensor_scalar(prob, expd, resum, None, ALU.mult))
                    link(nc.vector.reduce_max(m1, prob, AX.X))
                    link(nc.vector.scalar_tensor_tensor(t1, prob, m1, order[:, :], ALU.is_equal, ALU.mult))
                    link(nc.vector.reduce_max(w1, t1, AX.X))
                    link(nc.vector.tensor_scalar(f1, t1, w1, None, ALU.is_equal))
                    link(nc.vector.scalar_tensor_tensor(p2, f1, -2.0, prob, ALU.mult, ALU.add))
                    link(nc.vector.reduce_max(m2, p2, AX.X))
                    link(nc.vector.scalar_tensor_tensor(t2, p2, m2, order[:, :], ALU.is_equal, ALU.mult))
                    link(nc.vector.reduce_max(w2, t2, AX.X))
                    link(nc.vector.scalar_tensor_tensor(f2, t2, w2, f1, ALU.is_equal, ALU.add))
                    wait(dve, g_ps, t - 1)
                    nc.vector.tensor_tensor(gate[j % 2][:, 0:NR], prob, f2, ALU.mult).then_inc(gate_ok, 1)
                    dve.wait_ge(gate_ok, t + 1)

                def gather(k, j, c):
                    t = k * G + j
                    even, odd = acc[j % 2][:, 0, :], acc[j % 2][:, 1, :]
                    dve.wait_ge(e_ps, t * 9 + c + 1)
                    bank = ps_e[c % 3]
                    if c == NR // 2:
                        dve.wait_ge(e_ok, t * STEPS + NR - 1)
                        nc.vector.tensor_tensor(even, bank[:, 0:D], even, ALU.add).then_inc(e_ok, 1)
                        dve.wait_ge(e_ok, t * STEPS + NR + 1)
                        nc.vector.tensor_tensor(even, even, odd, ALU.add).then_inc(e_ok, 1)
                        return
                    for h in range(2):
                        e = 2 * c + h
                        weighed, by = bank[:, h * D:(h + 1) * D], gate[j % 2][:, e:e + 1]
                        if e == 1:
                            nc.vector.tensor_scalar(odd, weighed, by, None, ALU.mult).then_inc(e_ok, 1)
                            continue
                        if e > 1:
                            dve.wait_ge(e_ok, t * STEPS + e - 1)
                        own = odd if h else even
                        nc.vector.scalar_tensor_tensor(own, weighed, by, own, ALU.mult, ALU.add).then_inc(e_ok, 1)

                for j in range(G):
                    scaled(0, j)
                residual(0, 0)
                centred(0, 0)
                highest(0, 0)
                choose(0, 0)
                start = count[0]
                per = [0]

                def emit(k):
                    if not isinstance(k, int) or k:
                        count[0] = start + k * per[0]
                    for j in range(G):
                        nk, nj = (k, j + 1) if j < G - 1 else (k + 1, 0)
                        more = not final(k, j)
                        if more:
                            residual(nk, nj)
                        gather(k, j, 0)
                        gather(k, j, 1)
                        if more:
                            centred(nk, nj)
                        gather(k, j, 2)
                        gather(k, j, 3)
                        gather(k, j, 4)
                        if more:
                            highest(nk, nj)
                        gather(k, j, 5)
                        if more:
                            choose(nk, nj)
                        for c in range(6, 9):
                            gather(k, j, c)
                        if not (isinstance(k, int) and k == GPB - 1) and j < G - 1:
                            scaled(k + 1, j)
                            if j == G - 2:
                                scaled(k + 1, j + 1)
                    if isinstance(k, int) and k == 0:
                        per[0] = count[0] - start

                blocks(dve, emit)


_INS = ['L0_attn_x', 'L0_attn_w_qkv', 'L0_attn_b_qkv', 'L0_attn_w_out', 'L0_attn_b_out', 'L0_ffn_centroids',
        'L0_ffn_expert_biases', 'L0_ffn_Wr', 'L0_ffn_br', 'L0_ffn_Ws', 'L0_ffn_bs']
_OUTS = [((2, 2048, 256), 'float32')]


def kernel(**inputs):
    import numpy as _np
    import concourse.bacc as _bacc
    from concourse import mybir as _mybir
    from concourse.bass_utils import run_bass_kernel_spmd as _run

    nc = _bacc.Bacc("TRN2", target_bir_lowering=False, num_devices=1)
    arrays, args = {}, []
    for name in _INS:
        a = _np.ascontiguousarray(inputs[name])
        arrays[f"in_{name}_dram"] = a
        args.append(nc.dram_tensor(f"in_{name}_dram", a.shape, _mybir.dt.from_np(a.dtype), kind="ExternalInput").ap())
    for i, (shape, dtype) in enumerate(_OUTS):
        dt = _mybir.dt.from_np(_np.dtype(dtype))
        args.append(nc.dram_tensor(f"out_{i}_dram", shape, dt, kind="ExternalOutput").ap())
    pre_ln_arccos_attention_moe_kernel(nc, *args)
    r = _run(nc, [arrays], core_ids=[0])
    return r.results[0]["out_0_dram"]
```
